# Optimizing a Trainium2 kernel written in Bass

```python
import numpy as np
import jax
import jax.numpy as jnp

def _softmax(x, axis=-1):
    return jax.nn.softmax(x, axis=axis)

def _gelu(x):
    return jax.nn.gelu(x, approximate=True)

def _silu(x):
    return jax.nn.silu(x)

def _sigmoid(x):
    return jax.nn.sigmoid(x)

def _layernorm(x, axis=-1, eps=1e-05):
    m = jnp.mean(x, axis=axis, keepdims=True)
    v = jnp.var(x, axis=axis, keepdims=True)
    return (x - m) / jnp.sqrt(v + eps)

def _scatter_add(tgt, idx, src, axis=0):
    return tgt.at[idx].add(src)

def _segment_sum(src, seg, n):
    return jax.ops.segment_sum(src, seg, n)
kernel_name = 'mk_flamingo_gated_d1_seqx_r8_348f5e'

def setup_inputs(seed: int=0):
    np.random.seed(seed)
    _w = jnp.asarray

    def _rec_inputs():
        import jax
        import jax.numpy as jnp
        _rk = jax.random.key(seed)
        x = 0.0003765 + 1 * jax.random.normal(jax.random.fold_in(_rk, 1), (8, 128, 256), jnp.float32)
        _lenS = 128 - jax.random.randint(jax.random.fold_in(_rk, 7), (8,), 0, max(1, 128 // 4) + 1, jnp.int32)
        _lenS2 = 128 - jax.random.randint(jax.random.fold_in(_rk, 8), (8,), 0, max(1, 128 // 4) + 1, jnp.int32)
        _ctx_2048P = jax.random.normal(jax.random.fold_in(_rk, 11), (8, 16, 256), jnp.float32)
        _ctx_2048c = jax.random.dirichlet(jax.random.fold_in(_rk, 511), 0.3 * jnp.ones((16,), jnp.float32), (8, 128))
        _ctx_2048t = jnp.einsum('bsk,bkd->bsd', _ctx_2048c, _ctx_2048P)
        _ctx_2048t = _ctx_2048t * jax.lax.rsqrt(jnp.mean(jnp.square(_ctx_2048t)) + 1e-12) * 0.953939
        ctx_2048 = -0.000292821 + 1.00034 * (_ctx_2048t + 0.3 * jax.random.normal(jax.random.fold_in(_rk, 611), (8, 128, 256), jnp.float32))
        _g = jax.random.normal(jax.random.fold_in(_rk, 9001), (2, 1), jnp.float32)
        _g = jnp.sign(_g) * jnp.maximum(jnp.abs(_g), 1.0) + (_g == 0) * 1.0
        g_xattn = _g[0]
        g_ffn = _g[1]
        return (x, ctx_2048, g_xattn, g_ffn)
    x, ctx_2048, g_xattn, g_ffn = _rec_inputs()

    def _L0_xattn_setup():
        import jax, jax.numpy as jnp
        import numpy as np
        key = jax.random.key(seed)
        k1, k2, k3, k4, k5 = jax.random.split(key, 5)
        B, D_MODEL, L = (2, 128, 256)
        HEAD_DIM = 8
        H = D_MODEL // HEAD_DIM
        return {'k': jax.random.normal(k1, (B, D_MODEL, L), dtype=jnp.float32), 'v': jax.random.normal(k2, (B, D_MODEL, L), dtype=jnp.float32), 'q': jax.random.normal(k3, (B, D_MODEL, L), dtype=jnp.float32), 'ssm_kernel': jax.random.normal(k4, (H, L), dtype=jnp.float32), 'D': jax.random.normal(k5, (H,), dtype=jnp.float32), 'head_dim': HEAD_DIM}
    _L0_xattn_all = _L0_xattn_setup()
    _L0_xattn_in = {k: v for k, v in _L0_xattn_all.items() if k in ('ssm_kernel', 'D')}
    del _L0_xattn_all

    def _L0_ffn_setup():
        import jax, jax.numpy as jnp
        import numpy as np
        B, S, H, E, D, K = (2, 256, 256, 8, 256, 2)
        key = jax.random.key(seed)
        ks = jax.random.split(key, 4)
        return {'x': jax.random.normal(ks[0], (B, S, H), jnp.float32), 'router_w': jax.random.normal(ks[1], (H, E), jnp.float32) / np.sqrt(H).astype(np.float32), 'router_b': jnp.zeros((E,), jnp.float32), 'expert_w': jax.random.normal(ks[2], (E, H, D), jnp.float32) / np.sqrt(H).astype(np.float32), 'expert_b': jnp.zeros((E, D), jnp.float32), 'out_w': jax.random.normal(ks[3], (D, D), jnp.float32) / np.sqrt(D).astype(np.float32), 'out_b': jnp.zeros((D,), jnp.float32)}
    _L0_ffn_all = _L0_ffn_setup()
    _L0_ffn_in = {k: v for k, v in _L0_ffn_all.items() if k in ('router_w', 'router_b', 'expert_w', 'expert_b', 'out_w', 'out_b')}
    del _L0_ffn_all
    return {'x': x, 'ctx_2048': ctx_2048, 'g_xattn': g_xattn, 'g_ffn': g_ffn, 'L0_xattn_ssm_kernel': _L0_xattn_in['ssm_kernel'], 'L0_xattn_D': _L0_xattn_in['D'], 'L0_ffn_router_w': _L0_ffn_in['router_w'], 'L0_ffn_router_b': _L0_ffn_in['router_b'], 'L0_ffn_expert_w': _L0_ffn_in['expert_w'], 'L0_ffn_expert_b': _L0_ffn_in['expert_b'], 'L0_ffn_out_w': _L0_ffn_in['out_w'], 'L0_ffn_out_b': _L0_ffn_in['out_b']}

def reference(x, ctx_2048, g_xattn, g_ffn, L0_xattn_ssm_kernel, L0_xattn_D, L0_ffn_router_w, L0_ffn_router_b, L0_ffn_expert_w, L0_ffn_expert_b, L0_ffn_out_w, L0_ffn_out_b):
    import jax
    import jax.numpy as jnp

    def _L0_xattn_ref(k, v, q, ssm_kernel, D, head_dim):
        import jax, jax.numpy as jnp
        import numpy as np
        B, HD, L = k.shape
        H = HD // head_dim
        fft_size = 2 * L
        k_ = k.reshape(B, H, head_dim, L)
        v_ = v.reshape(B, H, head_dim, L)
        q_ = q.reshape(B, H, head_dim, L)
        kv = jnp.einsum('bhil,bhjl->bijhl', k_, v_)
        kv_f = jnp.fft.rfft(kv, n=fft_size)
        kernel_f = jnp.fft.rfft(ssm_kernel, n=fft_size)
        y = jnp.fft.irfft(kv_f * kernel_f, n=fft_size)[..., :L]
        out = y + kv * D[None, None, None, :, None]
        out = jnp.einsum('bijhl,bhil->bjhl', out, q_)
        out = jnp.transpose(out, (0, 2, 1, 3)).reshape(B, H * head_dim, L)
        return out.astype(k.dtype)

    def _L0_ffn_ref(x, router_w, router_b, expert_w, expert_b, out_w, out_b):
        import jax, jax.numpy as jnp
        import numpy as np
        B, S, H, E, D, K = (2, 256, 256, 8, 256, 2)
        num_experts = expert_w.shape[0]
        router_logits = jnp.einsum('bsh,he->bse', x, router_w) + router_b
        router_probs = jax.nn.softmax(router_logits, axis=-1)
        top_k_probs, top_k_indices = jax.lax.top_k(router_probs, K)
        top_k_probs = top_k_probs / jnp.sum(top_k_probs, axis=-1, keepdims=True)
        onehot = jax.nn.one_hot(top_k_indices, num_experts, dtype=x.dtype)
        gates = jnp.einsum('bsk,bske->bse', top_k_probs, onehot)
        expert_out = jax.nn.gelu(jnp.einsum('bsh,ehd->ebsd', x, expert_w) + expert_b[:, None, None, :])
        combined = jnp.einsum('bse,ebsd->bsd', gates, expert_out)
        return jnp.einsum('bsd,df->bsf', combined, out_w) + out_b
    x = x + jnp.tanh(g_xattn[0]) * _L0_xattn_ref(ctx_2048, ctx_2048, _layernorm(x, axis=-1), L0_xattn_ssm_kernel, L0_xattn_D, 8)
    x = x + jnp.tanh(g_ffn[0]) * _L0_ffn_ref(_layernorm(x, axis=-1), L0_ffn_router_w, L0_ffn_router_b, L0_ffn_expert_w, L0_ffn_expert_b, L0_ffn_out_w, L0_ffn_out_b)
    return x

_drawn_inputs = setup_inputs


def setup_inputs(seed=0):
    import zlib

    import numpy as np

    out = dict(_drawn_inputs(seed))
    spreads = {'L0_ffn_router_b': (0.0, 0.8), 'L0_ffn_expert_b': (0.0, 0.8), 'L0_ffn_out_b': (0.0, 2.0)}
    factors = {'L0_ffn_router_w': 4.349, 'L0_ffn_expert_w': 3.868, 'L0_ffn_out_w': 3.245}
    for name, (base, spread) in spreads.items():
        noise = np.random.default_rng([zlib.crc32(name.encode()), seed]).standard_normal(out[name].shape)
        drawn = base * np.exp(spread * noise) if base else spread * noise
        out[name] = jnp.asarray(drawn.astype(out[name].dtype))
    for name, factor in factors.items():
        out[name] = (out[name] * factor).astype(out[name].dtype)
    return out
```

```python
from contextlib import ExitStack

import concourse.bass as bass
from concourse import mybir

F32 = mybir.dt.float32
F32R = mybir.dt.float32r
U32 = mybir.dt.uint32
ALU = mybir.AluOpType
ACT = mybir.ActivationFunctionType

P = 128
HD = 8
HB = HD // 2
EPS = 1e-5
RING = 4
SLOTS = 8
RAW = 4
GB = 4
LOADS = 4
POOLSUB = 8


def flamingo_kernel(nc, x, ctx_in, g_xattn, g_ffn, ssm_kernel, ssm_d, router_w, router_b, expert_w, expert_b,
                    out_w, out_b, out):
    B, S, L = x.shape
    H = ssm_kernel.shape[0]
    E = expert_w.shape[0]
    C = L // P
    G = 2
    BG = B // G
    CB = C * BG
    NP = HD * HD - HB * HB
    NPU = HB * HD
    BL = B // LOADS
    HL = H // LOADS
    EP = E // 2
    assert S == P and H * HD == P and L == C * P and C == 2 and E * 4 * L * 4 <= 16 * 2048

    with ExitStack() as stack:
        def sb(name, shape, dt=F32):
            return stack.enter_context(nc.sbuf_tensor(name, shape, dt))

        def sem(name):
            return stack.enter_context(nc.semaphore(name))

        x_t = sb("x_t", [P, B * L])
        ctx_t = sb("ctx_t", [P, B * L])
        q_t = sb("q_t", [P, B * L])
        ctxT_t = sb("ctxT_t", [P, G * CB * P])
        qT_t = sb("qT_t", [P, G * CB * P])
        kv_t = sb("kv_t", [P, SLOTS * CB * NP])
        toep_t = sb("toep_t", [P, H * L])
        zq_t = sb("zq_t", [P, G * CB * HD * P])
        w_hi_t = sb("w_hi_t", [P, C * E * L], F32R)
        w_lo_t = sb("w_lo_t", [P, C * E * L], F32R)
        zT_hi_t = sb("zT_hi_t", [P, B * C * P], F32R)
        zT_lo_t = sb("zT_lo_t", [P, B * C * P], F32R)
        gelu_t = sb("gelu_t", [P, GB * 2 * L])
        mix_t = sb("mix_t", [P, 2 * 2 * L])
        mixT_t = sb("mixT_t", [P, C * P])
        ow_t = sb("ow_t", [P, C * L])
        obias = sb("obias", [P, L])
        rw_t = sb("rw_t", [P, C * E])
        rwlast = sb("rwlast", [P, E])
        rw_hi = sb("rw_hi", [P, C * E], F32R)
        rw_lo = sb("rw_lo", [P, C * E], F32R)
        ident = sb("ident", [P, P])
        taps = sb("taps", [H, L])
        kpad = sb("kpad", [H, L + P])
        dcol = sb("dcol", [H, 1])
        gains = sb("gains", [P, 2])
        tgains = sb("tgains", [P, 2])
        halfg = sb("halfg", [P, 2])
        neghalf = sb("neghalf", [P, BG])
        stats = sb("stats", [P, B * 6])
        mv = sb("mv", [P, 2 * B * 2])
        vareps = sb("vareps", [P, 2 * B])
        rstd = sb("rstd", [P, 2 * B])
        qscale = sb("qscale", [P, B])
        lgT_sb = sb("lgT_sb", [E, BG * P])
        lg = sb("lg", [P, BG * E])
        top = sb("top", [P, BG * 8])
        topi = sb("topi", [P, BG * 8], U32)
        topf = sb("topf", [P, BG * 2])
        gap = sb("gap", [P, BG])
        tgap = sb("tgap", [P, BG])
        gate2 = sb("gate2", [P, 2 * BG])
        eids = sb("eids", [P, E])
        hit = sb("hit", [P, 2 * BG * E])
        gates_t = sb("gates_t", [P, B * E])
        scratch = nc.dram_tensor("kpad_dram", [H, L + P], F32, kind="Internal").ap()

        xv = x_t[:, :].rearrange("p (b l) -> p b l", b=B)
        cv = ctx_t[:, :].rearrange("p (b l) -> p b l", b=B)
        qv = q_t[:, :].rearrange("p (b l) -> p b l", b=B)
        ctxT = ctxT_t[:, :].rearrange("p (g c b n) -> p g c b n", g=G, c=C, b=BG)
        qT = qT_t[:, :].rearrange("p (g c b n) -> p g c b n", g=G, c=C, b=BG)
        ctxTm = ctxT_t[:, :].rearrange("p (g a n) -> p g a n", g=G, a=CB)
        qTm = qT_t[:, :].rearrange("p (g a n) -> p g a n", g=G, a=CB)
        kv = kv_t[:, :].rearrange("p (s a n) -> p s a n", s=SLOTS, a=CB)
        toep = toep_t[:, :].rearrange("p (h l) -> p h l", h=H)
        zq = zq_t[:, :].rearrange("p (g a i n) -> p g a i n", g=G, a=CB, i=HD)
        w_hi = w_hi_t[:, :].rearrange("p (c e n) -> p c e n", c=C, e=E)
        w_lo = w_lo_t[:, :].rearrange("p (c e n) -> p c e n", c=C, e=E)
        zT_hi = zT_hi_t[:, :].rearrange("p (b c n) -> p b c n", b=B, c=C)
        zT_lo = zT_lo_t[:, :].rearrange("p (b c n) -> p b c n", b=B, c=C)
        raw = ctx_t[:, :].rearrange("p (r c n) -> p r c n", r=RAW, c=C)
        wlast = q_t[:, 0:E * L].rearrange("p (e n) -> p e n", e=E)
        gelu = gelu_t[:, :].rearrange("p (s e n) -> p s e n", s=GB, e=2)
        mix = mix_t[:, :].rearrange("p (s k n) -> p s k n", s=2, k=2)
        mixT = mixT_t[:, :].rearrange("p (c n) -> p c n", c=C)
        ow = ow_t[:, :].rearrange("p (c n) -> p c n", c=C)
        rw = rw_t[:, :].rearrange("p (c n) -> p c n", c=C)
        lgv = lg[:, :].rearrange("p (b e) -> p b e", b=BG)
        topv = top[:, :].rearrange("p (b e) -> p b e", b=BG)
        topiv = topi[:, :].rearrange("p (b e) -> p b e", b=BG)
        topfv = topf[:, :].rearrange("p (b k) -> p b k", b=BG)
        hitv = hit[:, :].rearrange("p (k b e) -> p k b e", k=2, b=BG)
        gates = gates_t[:, :].rearrange("p (b e) -> p b e", b=B)
        mvv = mv[:, :].rearrange("p (b k) -> p b k", k=2)

        ring = [stack.enter_context(nc.psum_tensor(f"ring{i}", [P, 512], F32)) for i in range(RING)]
        red = [stack.enter_context(nc.psum_tensor(f"red{i}", [P, 512], F32)) for i in range(2)]
        zbank = stack.enter_context(nc.psum_tensor("zbank", [P, 512], F32))
        obank = stack.enter_context(nc.psum_tensor("obank", [P, 512], F32))

        s_kin, s_scr, s_gin, s_rin, s_ob = sem("s_kin"), sem("s_scr"), sem("s_gin"), sem("s_rin"), sem("s_ob")
        s_ctx = [sem(f"s_ctxin{i}") for i in range(LOADS)]
        s_x = [sem(f"s_xin{i}") for i in range(LOADS)]
        s_toep = [sem(f"s_toep{i}") for i in range(LOADS)]
        s_wlast, s_ow = sem("s_wlast"), sem("s_ow")
        s_raw = [sem(f"s_raw{i}") for i in range(E)]
        s_wb = [sem(f"s_wb{i}") for i in range(E)]
        s_rb, s_out = sem("s_rb"), sem("s_out")
        s_zero, s_ident, s_const, s_kv = sem("s_zero"), sem("s_ident"), sem("s_const"), sem("s_kv")
        s_rstd, s_wrel, s_rrel, s_one, s_xb = sem("s_rstd"), sem("s_wrel"), sem("s_rrel"), sem("s_one"), sem("s_xb")
        s_cT, s_qTp, s_conv, s_sum, s_zTp = sem("s_cT"), sem("s_qTp"), sem("s_conv"), sem("s_sum"), sem("s_zTp")
        s_lgT, s_lgp, s_exp, s_mixp, s_proj = sem("s_lgT"), sem("s_lgp"), sem("s_exp"), sem("s_mixp"), sem("s_proj")
        s_tg, s_cTe, s_qTe, s_zhi, s_whi = sem("s_tg"), sem("s_cTe"), sem("s_qTe"), sem("s_zhi"), sem("s_whi")
        s_lgTe, s_lg, s_tgap, s_gelu, s_mixT = sem("s_lgTe"), sem("s_lg"), sem("s_tgap"), sem("s_gelu"), sem("s_mixT")
        s_kd, s_half, s_st, s_mv, s_ve, s_qs, s_q = (sem("s_kd"), sem("s_half"), sem("s_st"), sem("s_mv"),
                                                     sem("s_ve"), sem("s_qs"), sem("s_q"))
        s_zq, s_x1, s_z, s_zlo, s_wlo, s_rhl = (sem("s_zq"), sem("s_x1"), sem("s_z"), sem("s_zlo"), sem("s_wlo"),
                                                sem("s_rhl"))
        s_max, s_idx, s_gap, s_g, s_hit, s_gates = (sem("s_max"), sem("s_idx"), sem("s_gap"), sem("s_g"),
                                                    sem("s_hit"), sem("s_gates"))
        s_mix, s_y = sem("s_mix"), sem("s_y")

        block = stack.enter_context(nc.Block())

        def rows(src, b0, n):
            return src[b0:b0 + n].rearrange("b s l -> s b l")

        def everywhere(src, offset, n):
            return bass.AP(src.tensor, offset, [[0, P], [1, n]])

        def backwards(tensor, width, offset):
            return bass.AP(tensor, offset + P - 1, [[width, P], [P, C], [-1, P]])

        def gathered(eng, e):
            eng.wait_ge(s_wb[e], 16)

        @block.sync
        def _(sp):
            sp.dma_start(taps[:, :], ssm_kernel).then_inc(s_kin, 16)
            sp.dma_start(dcol[:, :], ssm_d.rearrange("(h a) -> h a", a=1)).then_inc(s_kin, 16)
            for i in range(2):
                sp.dma_start(cv[:, BL * i:BL * (i + 1), :], rows(ctx_in, BL * i, BL)).then_inc(s_ctx[i], 16)
            sp.wait_ge(s_kd, 1)
            sp.wait_ge(s_const, 1)
            sp.dma_start(scratch, kpad[:, :]).then_inc(s_scr, 16)
            sp.wait_ge(s_scr, 16)
            for i in range(LOADS):
                src = bass.AP(scratch.tensor, HL * i * (P + L), [[1, P], [P + L, HL], [1, L]])
                sp.dma_start(toep[:, HL * i:HL * (i + 1), :], src).then_inc(s_toep[i], 16)
            sp.dma_start(rw_t[:, :].rearrange("p (c n) -> p c n", c=C),
                         router_w.rearrange("(c p) n -> p c n", c=C)).then_inc(s_rin, 16)
            sp.dma_start(rwlast[:, :], everywhere(router_w, (L - 1) * E, E)).then_inc(s_rin, 16)
            sp.dma_start(obias[:, :], everywhere(out_b, 0, L)).then_inc(s_ob, 16)
            sp.dma_start(ow, out_w.rearrange("(c p) n -> p c n", c=C)).then_inc(s_ow, 16)
            sp.wait_ge(s_rin, 32)
            sp.dma_start(rw_t[P - 1:P, E:2 * E], router_b.rearrange("(a n) -> a n", a=1)).then_inc(s_rb, 16)
            sp.wait_ge(s_qTp, B // BL)
            sp.dma_start(wlast, bass.AP(expert_w.tensor, (L - 1) * L, [[0, P], [L * L, E], [1, L]])).then_inc(s_wlast, 16)
            sp.wait_ge(s_cT, B // BL)
            for e in range(E + 2):
                if e < E:
                    if e >= RAW:
                        sp.wait_ge(s_whi, e - RAW + 1)
                        sp.wait_ge(s_wlo, e - RAW + 1)
                    sp.dma_start(raw[:, e % RAW], expert_w[e].rearrange("(c p) n -> p c n", c=C)).then_inc(s_raw[e], 16)
                if e >= 2:
                    sp.wait_ge(s_raw[e - 2], 16)
                    sp.dma_start(raw[P - 1:P, (e - 2) % RAW, 1, :], expert_b[e - 2:e - 1, :]).then_inc(s_wb[e - 2], 16)
            for b in range(B):
                sp.wait_ge(s_y, b + 1)
                sp.dma_start(out[b], xv[:, b, :]).then_inc(s_out, 16)
            sp.wait_ge(s_out, 16 * B)

        def products(pool, n):
            g, h = divmod(n, H)
            if n % H == 0:
                pool.wait_ge(s_cTe, (g + 1) * (BG // BL))
            if n >= SLOTS:
                pool.wait_ge(s_conv, n - SLOTS + 1)
            head = ctxTm[:, g, :, HD * h:HD * (h + 1)]
            lower = head[:, :, 0:HB]
            upper = head[:, :, HB:HD]
            dst = kv[:, n % SLOTS]
            pool.tensor_tensor(dst[:, :, 0:NPU].rearrange("p a (i j) -> p a i j", i=HB),
                               lower.unsqueeze(3).to_broadcast([P, CB, HB, HD]),
                               head.unsqueeze(2).to_broadcast([P, CB, HB, HD]), ALU.mult)
            pool.tensor_tensor(dst[:, :, NPU:NP].rearrange("p a (i j) -> p a i j", i=HB),
                               upper.unsqueeze(3).to_broadcast([P, CB, HB, HB]),
                               upper.unsqueeze(2).to_broadcast([P, CB, HB, HB]), ALU.mult).then_inc(s_kv, 1)

        def inverse_std(pool, n):
            pool.wait_ge(s_ve, n + 1)
            pool.tensor_tensor(rstd[:, BG * n:BG * (n + 1)], vareps[:, BG * n:BG * (n + 1)], neghalf[:, :],
                               ALU.pow).then_inc(s_rstd, 1)

        def relative(eng, e, done):
            if e == 0:
                eng.wait_ge(s_wlast, 16)
            gathered(eng, e)
            r = e % RAW
            eng.tensor_tensor(raw[:, r, 0, :], raw[:, r, 0, :], wlast[:, e, :], ALU.subtract)
            eng.tensor_tensor(raw[0:P - 1, r, 1, :], raw[0:P - 1, r, 1, :], wlast[0:P - 1, e, :],
                              ALU.subtract).then_inc(done, 1)

        @block.gpsimd
        def _(pool):
            pool.memset(kpad[:, L:L + P], 0.0).then_inc(s_const, 1)
            pool.memset(ident[:, :], 0.0).then_inc(s_zero, 1)
            pool.wait_ge(s_zero, 1)
            pool.affine_select(out=ident[:, :], in_=ident[:, :], compare_op=ALU.not_equal, fill=1.0, base=0,
                               pattern=[[-1, P]], channel_multiplier=1).then_inc(s_ident, 1)
            pool.memset(neghalf[:, :], -0.5).then_inc(s_zero, 1)
            pool.iota(eids[:, :], pattern=[[1, E]], base=0, channel_multiplier=0,
                      allow_small_or_imprecise_dtypes=True).then_inc(s_const, 1)
            pool.wait_ge(s_zero, 2)
            for n in range(2 * H):
                products(pool, n)
                if n == 1:
                    inverse_std(pool, 0)
                if n == 7:
                    inverse_std(pool, 1)
                if n == 9:
                    pool.wait_ge(s_rb, 16)
                    pool.tensor_tensor(rw[:, 0], rw[:, 0], rwlast[:, :], ALU.subtract)
                    pool.tensor_tensor(rw[0:P - 1, 1], rw[0:P - 1, 1], rwlast[0:P - 1, :],
                                       ALU.subtract).then_inc(s_rrel, 1)
                if 12 <= n < 12 + 2 * E and n % 2 == 0:
                    relative(pool, (n - 12) // 2, s_wrel)
                if n == 12 + 2 * E:
                    pool.wait_ge(s_wrel, E)
                    pool.memset(qv[:, :, L - 1:L], 1.0).then_inc(s_one, 1)
                    inverse_std(pool, 2)
            inverse_std(pool, 3)

            for b in range(B):
                if b == 0:
                    pool.wait_ge(s_half, 3)
                pool.wait_ge(s_z, b + 1)
                pool.tensor_tensor(xv[:, b, :], xv[:, b, :], obias[:, :], ALU.add).then_inc(s_xb, 1)

        @block.scalar
        def _(act):
            act.preload_act_table(ACT.Gelu_apprx_tanh)
            for i in range(2):
                act.dma_start(xv[:, BL * i:BL * (i + 1), :], rows(x, BL * i, BL)).then_inc(s_x[i], 16)
            act.dma_start(gains[:, 0:1], everywhere(g_xattn, 0, 1)).then_inc(s_gin, 16)
            act.dma_start(gains[:, 1:2], everywhere(g_ffn, 0, 1)).then_inc(s_gin, 16)
            for i in range(2, LOADS):
                act.dma_start(cv[:, BL * i:BL * (i + 1), :], rows(ctx_in, BL * i, BL)).then_inc(s_ctx[i], 16)
            for i in range(2, LOADS):
                act.dma_start(xv[:, BL * i:BL * (i + 1), :], rows(x, BL * i, BL)).then_inc(s_x[i], 16)

            def evacuate(dst, banks, ready, done, i):
                act.wait_ge(ready, i + 1)
                g, k = divmod(i, BG // BL)
                act.activation(dst[:, g, :, BL * k:BL * (k + 1), :].rearrange("p c b n -> p c (b n)"),
                               banks[i % 2][:, :].rearrange("p (c n) -> p c n", c=C), ACT.Copy).then_inc(done, 1)

            def split_weights(e):
                act.wait_ge(s_wrel, e + 1)
                act.activation(w_hi[:, :, e, :], raw[:, e % RAW], ACT.Copy).then_inc(s_whi, 1)

            def z_high(b):
                act.wait_ge(s_zTp, b + 1)
                act.activation(zT_hi[:, b].rearrange("p c n -> p (c n)"), zbank[:, 0:L], ACT.Copy).then_inc(s_zhi, 1)

            def route(g):
                act.wait_ge(s_lgT, g + 1)
                act.activation(lgT_sb[:, :], red[0][0:E, :], ACT.Copy).then_inc(s_lgTe, 1)
                act.wait_ge(s_lgp, g + 1)
                if g:
                    act.wait_ge(s_gates, g)
                act.activation(lg[:, :], red[1][:, 0:BG * E], ACT.Copy).then_inc(s_lg, 1)
                act.wait_ge(s_gap, g + 1)
                act.activation(tgap[:, :], gap[:, :], ACT.Tanh, scale=0.5).then_inc(s_tgap, 1)

            def activate(n):
                act.wait_ge(s_exp, n + 1)
                if n >= GB:
                    act.wait_ge(s_mix, 2 * (n - GB + 1))
                act.activation(gelu[:, n % GB].rearrange("p e n -> p (e n)"), ring[n % RING][:, :],
                               ACT.Gelu_apprx_tanh).then_inc(s_gelu, 1)

            def mixed(b):
                act.wait_ge(s_mixp, b + 1)
                if b:
                    act.wait_ge(s_proj, b)
                act.activation(mixT_t[:, :], obank[:, 0:C * P], ACT.Copy).then_inc(s_mixT, 1)

            for i in range(2):
                evacuate(ctxT, red, s_cT, s_cTe, i)
            act.wait_ge(s_gin, 32)
            act.activation(tgains[:, :], gains[:, :], ACT.Tanh).then_inc(s_tg, 1)
            for i in range(2):
                evacuate(qT, (zbank, obank), s_qTp, s_qTe, i)
            for i in range(2, LOADS):
                evacuate(ctxT, red, s_cT, s_cTe, i)
            for i in range(2, LOADS):
                evacuate(qT, (zbank, obank), s_qTp, s_qTe, i)
            for e in range(E):
                split_weights(e)
            for b in range(BG):
                z_high(b)
            for b in range(B):
                for k in range(EP):
                    activate(EP * b + k)
                    if (b, k) == (0, 0):
                        route(0)
                    if b and k == 1:
                        mixed(b - 1)
                    if b in (1, 2) and k in (1, 3):
                        z_high(BG + 2 * (b - 1) + k // 2)
                    if b == 3 and k == 1:
                        route(1)
            mixed(B - 1)

        @block.tensor
        def _(pe):
            pe.wait_ge(s_ident, 1)

            def transposed(src, banks, produced, i):
                for c in range(C):
                    for b in range(BL):
                        last = pe.transpose(banks[i % 2][:, P * (BL * c + b):P * (BL * c + b + 1)],
                                            src[:, BL * i + b, P * c:P * (c + 1)], ident[:, :])
                last.then_inc(produced, 1)

            def context(i):
                pe.wait_ge(s_ctx[i], 16)
                if i >= 2:
                    pe.wait_ge(s_cTe, i - 1)
                transposed(cv, red, s_cT, i)

            def queries(i):
                pe.wait_ge(s_q, BL * (i + 1))
                if i >= 2:
                    pe.wait_ge(s_qTe, i - 1)
                transposed(qv, (zbank, obank), s_qTp, i)

            def ring_free(n):
                last = n - RING
                if last >= 2 * H:
                    pe.wait_ge(s_gelu, last - 2 * H + 1)
                elif last >= 0:
                    pe.wait_ge(s_zq, last + 1)

            def convolve(n):
                g, h = divmod(n, H)
                if g == 0 and h % HL == 0:
                    pe.wait_ge(s_toep[h // HL], 16)
                pe.wait_ge(s_kv, n + 1)
                ring_free(n)
                half = BG * NP
                y = ring[n % RING]
                src = kv[:, n % SLOTS].rearrange("p (c b) n -> p c (b n)", c=C)
                within, before = toep[:, h, P:2 * P], toep[:, h, 0:P]
                pe.matmul(y[:, 0:half], within, src[:, 0], start=True, stop=True)
                pe.matmul(y[:, half:2 * half], before, src[:, 0], start=True, stop=False)
                pe.matmul(y[:, half:2 * half], within, src[:, 1], start=False, stop=True).then_inc(s_conv, 1)

            def sum_channels(b):
                g = b // BG
                if b % BG == 0:
                    pe.wait_ge(s_zq, (g + 1) * H)
                if b >= 2:
                    pe.wait_ge(s_x1, b - 1)
                if b == BG:
                    pe.wait_ge(s_lgTe, 1)
                if b == BG + 1:
                    pe.wait_ge(s_lg, 1)
                for c in range(C):
                    for i in range(HD):
                        last = pe.matmul(red[b % 2][:, P * c:P * (c + 1)], zq[:, g, BG * c + b % BG, i, :], ident[:, :],
                                         is_transpose=True, start=(i == 0), stop=(i == HD - 1))
                last.then_inc(s_sum, 1)

            def z_transposed(b):
                pe.wait_ge(s_z, b + 1)
                if b:
                    pe.wait_ge(s_zlo, b)
                for c in range(C):
                    last = pe.transpose(zbank[:, P * c:P * (c + 1)], qv[:, b, P * c:P * (c + 1)], ident[:, :])
                last.then_inc(s_zTp, 1)

            def route_logits(g):
                pe.wait_ge(s_rhl, 2)
                pe.wait_ge(s_zlo, BG * (g + 1))
                pe.wait_ge(s_x1, BG * (g + 1))
                own = slice(BG * g, BG * (g + 1))
                for c in range(C):
                    for n, (w, z) in enumerate(((rw_hi, zT_hi), (rw_hi, zT_lo), (rw_lo, zT_hi))):
                        last = pe.matmul(red[0][0:E, :], w[:, E * c:E * (c + 1)], z[:, own, c, :],
                                         start=(c == 0 and n == 0), stop=(c == C - 1 and n == 2))
                last.then_inc(s_lgT, 1)

            def route_rows(g):
                pe.wait_ge(s_lgTe, g + 1)
                for b in range(BG):
                    last = pe.transpose(red[1][:, E * b:E * (b + 1)], lgT_sb[:, P * b:P * (b + 1)], ident[0:E, 0:E])
                last.then_inc(s_lgp, 1)

            def experts(b, k):
                n = EP * b + k
                ring_free(2 * H + n)
                h = ring[n % RING]
                if b == 0:
                    pe.wait_ge(s_wlo, 2 * (k + 1))
                for c in range(C):
                    hi, lo = zT_hi[:, b, c, :], zT_lo[:, b, c, :]
                    whi = w_hi[:, c, 2 * k:2 * k + 2, :].rearrange("p e n -> p (e n)")
                    wlo = w_lo[:, c, 2 * k:2 * k + 2, :].rearrange("p e n -> p (e n)")
                    pe.matmul(h[:, :], hi, whi, start=(c == 0), stop=False)
                    pe.matmul(h[:, :], hi, wlo, start=False, stop=False)
                    last = pe.matmul(h[:, :], lo, whi, start=False, stop=(c == C - 1))
                last.then_inc(s_exp, 1)

            def mix_transposed(b):
                pe.wait_ge(s_mix, E * (b + 1))
                if b:
                    pe.wait_ge(s_y, b)
                else:
                    pe.wait_ge(s_qTe, LOADS)
                for c in range(C):
                    for k in range(2):
                        last = pe.matmul(obank[:, P * c:P * (c + 1)], mix[:, b % 2, k, P * c:P * (c + 1)], ident[:, :],
                                         is_transpose=True, start=(k == 0), stop=(k == 1))
                last.then_inc(s_mixp, 1)

            def project(b):
                if b == 0:
                    pe.wait_ge(s_ow, 16)
                pe.wait_ge(s_mixT, b + 1)
                for c in range(C):
                    last = pe.matmul(obank[:, L:2 * L], mixT[:, c, :], ow[:, c, :], start=(c == 0), stop=(c == C - 1))
                last.then_inc(s_proj, 1)

            for i in range(2):
                context(i)
            for i in range(2):
                queries(i)
            for n in range(H):
                convolve(n)
                if n == 2:
                    context(2)
                    context(3)
                if n == 5:
                    queries(2)
                    queries(3)
            for n in range(H, 2 * H):
                convolve(n)
                h = n - H
                if h in (2, 4, 6, 8):
                    sum_channels((h - 2) // 2)
                if h in (12, 13, 14, 15):
                    z_transposed(h - 12)
            experts(0, 0)
            route_logits(0)
            for b in range(B):
                for k in range(EP):
                    if (b, k) != (0, 0):
                        experts(b, k)
                    if (b, k) == (0, 1):
                        route_rows(0)
                    if b == 0 and k:
                        sum_channels(BG + k - 1)
                    if (b, k) == (1, 0):
                        sum_channels(B - 1)
                    if b and k == 1:
                        mix_transposed(b - 1)
                    if b and k == 2:
                        project(b - 1)
                    if b in (1, 2) and k in (1, 3):
                        z_transposed(BG + 2 * (b - 1) + k // 2)
                    if b == 3 and k == 0:
                        route_logits(1)
                    if b == 3 and k == 1:
                        route_rows(1)
            mix_transposed(B - 1)
            project(B - 1)

        @block.vector
        def _(dve):
            def statistics(b, n):
                dve.bn_stats(stats[:, 6 * b:6 * (b + 1)], xv[:, b, :]).then_inc(s_st, 1)
                dve.wait_ge(s_st, n + 1)
                dve.bn_aggr(mvv[:, n, :], stats[:, 6 * b:6 * (b + 1)]).then_inc(s_mv, 1)

            def add_eps(n):
                dve.wait_ge(s_mv, BG * (n + 1))
                dve.tensor_scalar(vareps[:, BG * n:BG * (n + 1)], mvv[:, BG * n:BG * (n + 1), 1], EPS, None,
                                  ALU.add).then_inc(s_ve, 1)

            def norm_x(g):
                for b in range(BG * g, BG * (g + 1)):
                    if b % BL == 0:
                        dve.wait_ge(s_x[b // BL], 16)
                    statistics(b, b)
                add_eps(g)

            def queries(g):
                own = slice(BG * g, BG * (g + 1))
                dve.wait_ge(s_rstd, g + 1)
                dve.wait_ge(s_tg, 1)
                dve.tensor_scalar(qscale[:, own], rstd[:, own], tgains[:, 0:1], None, ALU.mult).then_inc(s_qs, 1)
                dve.wait_ge(s_qs, g + 1)
                for b in range(BG * g, BG * (g + 1)):
                    dve.tensor_scalar(backwards(q_t, B * L, b * L), xv[:, b, :].rearrange("p (c n) -> p c n", c=C),
                                      mvv[:, b, 0:1], qscale[:, b:b + 1], ALU.subtract, ALU.mult).then_inc(s_q, 1)

            def query_products(n):
                g, h = divmod(n, H)
                if h == 0:
                    dve.wait_ge(s_qTe, (g + 1) * (BG // BL))
                dve.wait_ge(s_conv, n + 1)
                y = ring[n % RING][:, 0:CB * NP].rearrange("p (a n) -> p a n", a=CB)
                rows_lo = y[:, :, 0:NPU].rearrange("p a (i j) -> p a i j", i=HB)
                rows_hi = y[:, :, NPU:NP].rearrange("p a (i j) -> p a i j", i=HB)
                q = qTm[:, g, :, HD * h:HD * (h + 1)]
                dst = zq[:, g, :, :, HD * h:HD * (h + 1)]
                dve.tensor_tensor(dst[:, :, 0:HB, :], rows_lo, q[:, :, 0:HB].unsqueeze(3).to_broadcast([P, CB, HB, HD]),
                                  ALU.mult)
                q_hi = q[:, :, HB:HD].unsqueeze(3).to_broadcast([P, CB, HB, HB])
                dve.tensor_tensor(dst[:, :, HB:HD, HB:HD], rows_hi, q_hi, ALU.mult)
                dve.tensor_tensor(dst[:, :, HB:HD, 0:HB], rows_lo[:, :, :, HB:HD].rearrange("p a i j -> p a j i"), q_hi,
                                  ALU.mult).then_inc(s_zq, 1)

            def residual(b):
                dve.wait_ge(s_sum, b + 1)
                row = xv[:, b, :].rearrange("p (c n) -> p c n", c=C)
                dve.tensor_tensor(row, backwards(red[b % 2], 512, 0), row, ALU.add).then_inc(s_x1, 1)
                dve.wait_ge(s_x1, b + 1)
                statistics(b, B + b)

            def normalise(b):
                if b % BG == 0:
                    dve.wait_ge(s_rstd, 3 + b // BG)
                    dve.wait_ge(s_one, 1)
                dve.tensor_scalar(qv[:, b, 0:L - 1], xv[:, b, 0:L - 1], mvv[:, B + b, 0:1], rstd[:, B + b:B + b + 1],
                                  ALU.subtract, ALU.mult).then_inc(s_z, 1)

            def z_low(b):
                dve.wait_ge(s_zhi, b + 1)
                dve.tensor_tensor(zT_lo[:, b].rearrange("p c n -> p (c n)"), zbank[:, 0:L],
                                  zT_hi[:, b].rearrange("p c n -> p (c n)").bitcast(F32), ALU.subtract).then_inc(s_zlo, 1)

            def weights_low(e):
                dve.wait_ge(s_whi, e + 1)
                dve.tensor_tensor(w_lo[:, :, e, :], raw[:, e % RAW], w_hi[:, :, e, :].bitcast(F32),
                                  ALU.subtract).then_inc(s_wlo, 1)

            def router_split():
                dve.wait_ge(s_rrel, 1)
                dve.tensor_copy(rw_hi[:, :], rw_t[:, :]).then_inc(s_rhl, 1)
                dve.wait_ge(s_rhl, 1)
                dve.tensor_tensor(rw_lo[:, :], rw_t[:, :], rw_hi[:, :].bitcast(F32), ALU.subtract).then_inc(s_rhl, 1)

            def choose(g):
                dve.wait_ge(s_lg, g + 1)
                for b in range(BG):
                    dve.max(topv[:, b, :], lgv[:, b, :]).then_inc(s_max, 1)
                dve.wait_ge(s_max, BG * (g + 1))
                if g:
                    dve.wait_ge(s_tgap, g)
                dve.tensor_tensor(gap[:, :], topv[:, :, 0], topv[:, :, 1], ALU.subtract).then_inc(s_gap, 1)
                for b in range(BG):
                    last = dve.max_index(topiv[:, b, :], topv[:, b, :], lgv[:, b, :])
                last.then_inc(s_idx, 1)
                dve.wait_ge(s_idx, 2 * g + 1)
                dve.tensor_copy(topfv, topiv[:, :, 0:2]).then_inc(s_idx, 1)

            def weigh(g):
                dve.wait_ge(s_tgap, g + 1)
                dve.wait_ge(s_half, 2)
                dve.tensor_scalar(gate2[:, 0:BG], tgap[:, :], halfg[:, 0:1], halfg[:, 0:1], ALU.mult, ALU.add).then_inc(s_g, 1)
                dve.tensor_scalar(gate2[:, BG:2 * BG], tgap[:, :], halfg[:, 1:2], halfg[:, 0:1], ALU.mult,
                                  ALU.add).then_inc(s_g, 1)
                dve.wait_ge(s_idx, 2 * g + 2)
                for k in range(2):
                    dve.tensor_tensor(hitv[:, k], eids[:, :].unsqueeze(1).to_broadcast([P, BG, E]),
                                      topfv[:, :, k:k + 1].to_broadcast([P, BG, E]), ALU.is_equal).then_inc(s_hit, 1)
                dve.wait_ge(s_g, 2 * g + 2)
                dve.wait_ge(s_hit, 4 * g + 2)
                for k in range(2):
                    dve.tensor_tensor(hitv[:, k], hitv[:, k],
                                      gate2[:, BG * k:BG * (k + 1)].unsqueeze(2).to_broadcast([P, BG, E]),
                                      ALU.mult).then_inc(s_hit, 1)
                dve.wait_ge(s_hit, 4 * g + 4)
                dve.tensor_tensor(gates[:, BG * g:BG * (g + 1), :], hitv[:, 0], hitv[:, 1], ALU.add).then_inc(s_gates, 1)

            def accumulate(b, k):
                n = EP * b + k
                dve.wait_ge(s_gelu, n + 1)
                if k == 0 and b % BG == 0:
                    dve.wait_ge(s_gates, b // BG + 1)
                if k == 0 and b >= 2:
                    dve.wait_ge(s_mixp, b - 1)
                for e in range(2):
                    gate = gates[:, b, 2 * k + e:2 * k + e + 1]
                    acc = mix[:, b % 2, e, :]
                    if k == 0:
                        dve.tensor_scalar(acc, gelu[:, n % GB, e, :], gate, None, ALU.mult).then_inc(s_mix, 1)
                    else:
                        dve.wait_ge(s_mix, E * b + 2 * k + e - 1)
                        dve.scalar_tensor_tensor(out=acc, in0=gelu[:, n % GB, e, :], scalar=gate, in1=acc, op0=ALU.mult,
                                                 op1=ALU.add).then_inc(s_mix, 1)

            def finish(b):
                dve.wait_ge(s_proj, b + 1)
                dve.wait_ge(s_xb, b + 1)
                dve.tensor_tensor(xv[:, b, :], obank[:, L:2 * L], xv[:, b, :], ALU.add).then_inc(s_y, 1)

            dve.wait_ge(s_kin, 32)
            dve.tensor_copy(kpad[:, 0:L - 1], bass.AP(taps, L - 1, [[L, H], [-1, L - 1]]))
            dve.tensor_tensor(kpad[:, L - 1:L], taps[:, 0:1], dcol[:, :], ALU.add).then_inc(s_kd, 1)
            norm_x(0)
            queries(0)
            norm_x(1)
            dve.tensor_scalar(halfg[:, 0:1], tgains[:, 1:2], 0.5, None, ALU.mult).then_inc(s_half, 1)
            dve.tensor_scalar(halfg[:, 1:2], tgains[:, 1:2], -0.5, None, ALU.mult).then_inc(s_half, 1)
            dve.wait_ge(s_ob, 16)
            dve.tensor_scalar(obias[:, :], obias[:, :], tgains[:, 1:2], None, ALU.mult).then_inc(s_half, 1)
            for n in range(H):
                query_products(n)
                if n == 2:
                    queries(1)
                if n == 12:
                    router_split()
                if n == 14:
                    weights_low(0)
            for n in range(H, 2 * H):
                h = n - H
                query_products(n)
                if h in (3, 5, 7, 9):
                    residual((h - 3) // 2)
                if h == 9:
                    add_eps(2)
                if h % 2 == 0 and h <= 12:
                    weights_low(h // 2 + 1)
                if h == 10:
                    for b in range(BG):
                        normalise(b)
                if h >= 12:
                    z_low(h - 12)
            choose(0)
            weigh(0)
            for b in range(B):
                for k in range(EP):
                    accumulate(b, k)
                    if b == 0 and k:
                        residual(BG + k - 1)
                    if b == 1 and k == 0:
                        residual(B - 1)
                        add_eps(3)
                    if b == 1 and k == 1:
                        for s in range(BG, B):
                            normalise(s)
                    if b in (1, 2) and k in (1, 3):
                        z_low(BG + 2 * (b - 1) + k // 2)
                    if b == 3 and k == 1:
                        choose(1)
                        weigh(1)
                    if b and k == 3:
                        finish(b - 1)
            finish(B - 1)


_INS = ["x", "ctx_2048", "g_xattn", "g_ffn", "L0_xattn_ssm_kernel", "L0_xattn_D", "L0_ffn_router_w", "L0_ffn_router_b",
        "L0_ffn_expert_w", "L0_ffn_expert_b", "L0_ffn_out_w", "L0_ffn_out_b"]


def kernel(**inputs):
    import numpy as _np
    import concourse.bacc as _bacc
    from concourse import mybir as _mybir
    from concourse.bass_utils import run_bass_kernel_spmd as _run

    nc = _bacc.Bacc("TRN2", target_bir_lowering=False, num_devices=1)
    arrays, args = {}, []
    for name in _INS:
        a = _np.ascontiguousarray(inputs[name])
        arrays[f"in_{name}"] = a
        args.append(nc.dram_tensor(f"in_{name}", a.shape, _mybir.dt.from_np(a.dtype), kind="ExternalInput").ap())
    shape = inputs["x"].shape
    args.append(nc.dram_tensor("out_0", shape, _mybir.dt.float32, kind="ExternalOutput").ap())
    flamingo_kernel(nc, *args)
    r = _run(nc, [arrays], core_ids=[0])
    return r.results[0]["out_0"]
```

```python
from contextlib import ExitStack

import concourse.bass as bass
from concourse import mybir

F32 = mybir.dt.float32
F32R = mybir.dt.float32r
U32 = mybir.dt.uint32
ALU = mybir.AluOpType
ACT = mybir.ActivationFunctionType

P = 128
HD = 8
HB = HD // 2
EPS = 1e-5
RING = 4
SLOTS = 6
RAW = 4
GB = 4
LOADS = 4
WREL = (12, 14, 16, 18, 20, 22, 24, 26)
SUMS = (17, 18, 19, 20)
ZTS = (26, 27, 28, 29)
WREL = (14, 17, 20, 23)
LATE_SUMS = (1, 2, 3, 4)
LATE_ZTS = (8, 9, 10, 11)
MIXED = (14, 16, 18, 20, 22, 25, 29)
TOEP = ((0, 2), (2, 2), (4, 4), (8, 4), (12, 4))
DVE_EVERY = 4


def flamingo_kernel(nc, x, ctx_in, g_xattn, g_ffn, ssm_kernel, ssm_d, router_w, router_b, expert_w, expert_b,
                    out_w, out_b, out):
    B, S, L = x.shape
    H = ssm_kernel.shape[0]
    E = expert_w.shape[0]
    C = L // P
    G = 2
    BG = B // G
    CB = C * BG
    NP = HD * HD - HB * HB
    NPU = HB * HD
    BL = B // LOADS
    EP = E // 2
    assert S == P and H * HD == P and L == C * P and C == 2 and E * 4 * L * 4 <= 16 * 2048

    with ExitStack() as stack:
        def sb(name, shape, dt=F32):
            return stack.enter_context(nc.sbuf_tensor(name, shape, dt))

        def sem(name):
            return stack.enter_context(nc.semaphore(name))

        x_t = sb("x_t", [P, B * L])
        ctx_t = sb("ctx_t", [P, B * L])
        q_t = sb("q_t", [P, B * L])
        ctxT_t = sb("ctxT_t", [P, G * CB * P])
        qT_t = sb("qT_t", [P, G * CB * P])
        kv_t = sb("kv_t", [P, SLOTS * CB * NP])
        toep_t = sb("toep_t", [P, H * L])
        zq_t = sb("zq_t", [P, G * CB * HD * P])
        w_hi_t = sb("w_hi_t", [P, C * E * L], F32R)
        w_lo_t = sb("w_lo_t", [P, C * E * L], F32R)
        zT_hi_t = sb("zT_hi_t", [P, B * C * P], F32R)
        zT_lo_t = sb("zT_lo_t", [P, B * C * P], F32R)
        wlast_t = sb("wlast_t", [P, E * L])
        gelu_t = sb("gelu_t", [P, GB * 2 * L])
        mix_t = sb("mix_t", [P, BG * L])
        mixT_t = sb("mixT_t", [P, C * P])
        ow_t = sb("ow_t", [P, C * L])
        obias = sb("obias", [P, L])
        rw_t = sb("rw_t", [P, C * E])
        rwlast = sb("rwlast", [P, E])
        rw_hi = sb("rw_hi", [P, C * E], F32R)
        rw_lo = sb("rw_lo", [P, C * E], F32R)
        ident = sb("ident", [P, P])
        dcol = sb("dcol", [H, 1])
        gains = sb("gains", [P, 2])
        tgains = sb("tgains", [P, 2])
        halfg = sb("halfg", [P, 2])
        neghalf = sb("neghalf", [P, BG])
        stats = sb("stats", [P, B * 6])
        mv = sb("mv", [P, 2 * B * 2])
        vareps = sb("vareps", [P, 2 * B])
        rstd = sb("rstd", [P, 2 * B])
        qscale = sb("qscale", [P, B])
        lgT_sb = sb("lgT_sb", [E, BG * P])
        lg = sb("lg", [P, BG * E])
        top = sb("top", [P, BG * 8])
        topi = sb("topi", [P, BG * 8], U32)
        topf = sb("topf", [P, BG * 2])
        gap = sb("gap", [P, BG])
        tgap = sb("tgap", [P, BG])
        gate2 = sb("gate2", [P, 2 * BG])
        eids = sb("eids", [P, E])
        hit = sb("hit", [P, 2 * BG * E])
        gates_t = sb("gates_t", [P, B * E])
        scratch = nc.dram_tensor("kpad_dram", [H, L + P], F32, kind="Internal").ap()

        xv = x_t[:, :].rearrange("p (b l) -> p b l", b=B)
        cv = ctx_t[:, :].rearrange("p (b l) -> p b l", b=B)
        qv = q_t[:, :].rearrange("p (b l) -> p b l", b=B)
        ctxT = ctxT_t[:, :].rearrange("p (g c b n) -> p g c b n", g=G, c=C, b=BG)
        qT = qT_t[:, :].rearrange("p (g c b n) -> p g c b n", g=G, c=C, b=BG)
        ctxTm = ctxT_t[:, :].rearrange("p (g a n) -> p g a n", g=G, a=CB)
        qTm = qT_t[:, :].rearrange("p (g a n) -> p g a n", g=G, a=CB)
        kv = kv_t[:, :].rearrange("p (s a n) -> p s a n", s=SLOTS, a=CB)
        toep = toep_t[:, :].rearrange("p (h l) -> p h l", h=H)
        zq = zq_t[:, :].rearrange("p (g a i n) -> p g a i n", g=G, a=CB, i=HD)
        w_hi = w_hi_t[:, :].rearrange("p (c e n) -> p c e n", c=C, e=E)
        w_lo = w_lo_t[:, :].rearrange("p (c e n) -> p c e n", c=C, e=E)
        zT_hi = zT_hi_t[:, :].rearrange("p (b c n) -> p b c n", b=B, c=C)
        zT_lo = zT_lo_t[:, :].rearrange("p (b c n) -> p b c n", b=B, c=C)
        raw = ctx_t[:, :].rearrange("p (r c n) -> p r c n", r=RAW, c=C)
        wlast = wlast_t[:, :].rearrange("p (e n) -> p e n", e=E)
        gelu = gelu_t[:, :].rearrange("p (s e n) -> p s e n", s=GB, e=2)
        mix = mix_t[:, :].rearrange("p (s n) -> p s n", s=BG)
        taps, kpad = mix_t[0:H, 0:L], mix_t[0:H, L:2 * L + P]
        mixT = mixT_t[:, :].rearrange("p (c n) -> p c n", c=C)
        ow = ow_t[:, :].rearrange("p (c n) -> p c n", c=C)
        rw = rw_t[:, :].rearrange("p (c n) -> p c n", c=C)
        lgv = lg[:, :].rearrange("p (b e) -> p b e", b=BG)
        topv = top[:, :].rearrange("p (b e) -> p b e", b=BG)
        topiv = topi[:, :].rearrange("p (b e) -> p b e", b=BG)
        topfv = topf[:, :].rearrange("p (b k) -> p b k", b=BG)
        hitv = hit[:, :].rearrange("p (k b e) -> p k b e", k=2, b=BG)
        gates = gates_t[:, :].rearrange("p (b e) -> p b e", b=B)
        mvv = mv[:, :].rearrange("p (b k) -> p b k", k=2)

        ring = [stack.enter_context(nc.psum_tensor(f"ring{i}", [P, 512], F32)) for i in range(RING)]
        red = [stack.enter_context(nc.psum_tensor(f"red{i}", [P, 512], F32)) for i in range(2)]
        zbank = stack.enter_context(nc.psum_tensor("zbank", [P, 512], F32))
        obank = stack.enter_context(nc.psum_tensor("obank", [P, 512], F32))

        zbanks = (zbank, red[1])
        s_kin, s_scr, s_gin, s_rin, s_ob = sem("s_kin"), sem("s_scr"), sem("s_gin"), sem("s_rin"), sem("s_ob")
        s_ctx = [sem(f"s_ctxin{i}") for i in range(LOADS)]
        s_x = [sem(f"s_xin{i}") for i in range(LOADS)]
        s_toep = [sem(f"s_toep{i}") for i in range(len(TOEP))]
        s_wlast, s_ow = sem("s_wlast"), sem("s_ow")
        s_raw = [sem(f"s_raw{i}") for i in range(E)]
        s_wb = [sem(f"s_wb{i}") for i in range(E)]
        s_rb, s_out = sem("s_rb"), sem("s_out")
        s_zero, s_ident, s_const, s_kv = sem("s_zero"), sem("s_ident"), sem("s_const"), sem("s_kv")
        s_kvd = sem("s_kvd")
        s_rstd, s_wrel, s_rrel, s_one, s_xb = sem("s_rstd"), sem("s_wrel"), sem("s_rrel"), sem("s_one"), sem("s_xb")
        s_cT, s_qTp, s_conv, s_sum, s_zTp = sem("s_cT"), sem("s_qTp"), sem("s_conv"), sem("s_sum"), sem("s_zTp")
        s_lgT, s_lgp, s_exp, s_mixp, s_proj = sem("s_lgT"), sem("s_lgp"), sem("s_exp"), sem("s_mixp"), sem("s_proj")
        s_tg, s_cTe, s_qTe, s_zhi, s_whi = sem("s_tg"), sem("s_cTe"), sem("s_qTe"), sem("s_zhi"), sem("s_whi")
        s_lgTe, s_lg, s_tgap, s_gelu, s_mixT = sem("s_lgTe"), sem("s_lg"), sem("s_tgap"), sem("s_gelu"), sem("s_mixT")
        s_kd, s_half, s_st, s_mv, s_ve, s_qs, s_q = (sem("s_kd"), sem("s_half"), sem("s_st"), sem("s_mv"),
                                                     sem("s_ve"), sem("s_qs"), sem("s_q"))
        s_zq, s_x1, s_z, s_zlo, s_wlo, s_rhl = (sem("s_zq"), sem("s_x1"), sem("s_z"), sem("s_zlo"), sem("s_wlo"),
                                                sem("s_rhl"))
        s_max, s_idx, s_gap, s_g, s_hit, s_gates = (sem("s_max"), sem("s_idx"), sem("s_gap"), sem("s_g"),
                                                    sem("s_hit"), sem("s_gates"))
        s_mix, s_y = sem("s_mix"), sem("s_y")

        block = stack.enter_context(nc.Block())

        BLOCKS = [(b, k) for k in range(EP) for b in range(BG)] + [(b, k) for b in range(BG, B) for k in range(EP)]

        def added(b, k):
            return 2 * BLOCKS.index((b, k)) + 2

        def rows(src, b0, n):
            return src[b0:b0 + n].rearrange("b s l -> s b l")

        def load(eng, dst, src, done, i):
            eng.dma_start(dst[:, BL * i:BL * (i + 1), :], rows(src, BL * i, BL)).then_inc(done[i], 16)

        def everywhere(src, offset, n):
            return bass.AP(src.tensor, offset, [[0, P], [1, n]])

        def backwards(tensor, width, offset):
            return bass.AP(tensor, offset + P - 1, [[width, P], [P, C], [-1, P]])

        def raw_weights(sp, e):
            if e >= RAW:
                sp.wait_ge(s_whi, e - RAW + 1)
                sp.wait_ge(s_wlo, e - RAW + 1)
            sp.dma_start(raw[:, e % RAW], expert_w[e].rearrange("(c p) n -> p c n", c=C)).then_inc(s_raw[e], 16)

        def raw_bias(sp, e):
            sp.wait_ge(s_raw[e], 16)
            sp.dma_start(raw[P - 1:P, e % RAW, 1, :], expert_b[e:e + 1, :]).then_inc(s_wb[e], 16)

        @block.sync
        def _(sp):
            sp.dma_start(taps[:, :], ssm_kernel).then_inc(s_kin, 16)
            sp.dma_start(dcol[:, :], ssm_d.rearrange("(h a) -> h a", a=1)).then_inc(s_kin, 16)
            sp.wait_ge(s_kd, 1)
            sp.wait_ge(s_const, 1)
            sp.dma_start(scratch, kpad[:, :]).then_inc(s_scr, 16)
            sp.wait_ge(s_scr, 16)
            for i, (h, n) in enumerate(TOEP):
                src = bass.AP(scratch.tensor, h * (P + L), [[1, P], [P + L, n], [1, L]])
                sp.dma_start(toep[:, h:h + n, :], src).then_inc(s_toep[i], 16)
                if i == 1:
                    load(sp, cv, ctx_in, s_ctx, 2)
                    load(sp, cv, ctx_in, s_ctx, 3)
            for i in range(2, LOADS):
                load(sp, xv, x, s_x, i)
            sp.dma_start(wlast, bass.AP(expert_w.tensor, (L - 1) * L, [[0, P], [L * L, E], [1, L]])).then_inc(s_wlast, 16)
            sp.dma_start(rw_t[:, :].rearrange("p (c n) -> p c n", c=C),
                         router_w.rearrange("(c p) n -> p c n", c=C)).then_inc(s_rin, 16)
            sp.dma_start(rwlast[:, :], everywhere(router_w, (L - 1) * E, E)).then_inc(s_rin, 16)
            sp.dma_start(obias[:, :], everywhere(out_b, 0, L)).then_inc(s_ob, 16)
            sp.dma_start(ow, out_w.rearrange("(c p) n -> p c n", c=C)).then_inc(s_ow, 16)
            sp.wait_ge(s_rin, 32)
            sp.dma_start(rw_t[P - 1:P, E:2 * E], router_b.rearrange("(a n) -> a n", a=1)).then_inc(s_rb, 16)
            sp.wait_ge(s_cT, B // BL)
            for e in range(RAW):
                raw_weights(sp, e)
            for e in range(RAW):
                raw_bias(sp, e)
            raw_weights(sp, RAW)
            for e in range(RAW + 1, E):
                raw_weights(sp, e)
                raw_bias(sp, e - 1)
            raw_bias(sp, E - 1)
            for b in range(B):
                sp.wait_ge(s_y, b + 1)
                sp.dma_start(out[b], xv[:, b, :]).then_inc(s_out, 16)
            sp.wait_ge(s_out, 16 * B)

        def by_vector(n):
            return n % DVE_EVERY == 0

        def products(eng, n, done):
            g, h = divmod(n, H)
            if n % H < DVE_EVERY:
                eng.wait_ge(s_cTe, (g + 1) * (BG // BL))
            if n >= SLOTS:
                eng.wait_ge(s_conv, n - SLOTS + 1)
            head = ctxTm[:, g, :, HD * h:HD * (h + 1)]
            lower = head[:, :, 0:HB]
            upper = head[:, :, HB:HD]
            dst = kv[:, n % SLOTS]
            eng.tensor_tensor(dst[:, :, 0:NPU].rearrange("p a (i j) -> p a i j", i=HB),
                               lower.unsqueeze(3).to_broadcast([P, CB, HB, HD]),
                               head.unsqueeze(2).to_broadcast([P, CB, HB, HD]), ALU.mult)
            eng.tensor_tensor(dst[:, :, NPU:NP].rearrange("p a (i j) -> p a i j", i=HB),
                               upper.unsqueeze(3).to_broadcast([P, CB, HB, HB]),
                               upper.unsqueeze(2).to_broadcast([P, CB, HB, HB]), ALU.mult).then_inc(done, 1)

        def inverse_std(pool, n):
            pool.wait_ge(s_ve, n + 1)
            pool.tensor_tensor(rstd[:, BG * n:BG * (n + 1)], vareps[:, BG * n:BG * (n + 1)], neghalf[:, :],
                               ALU.pow).then_inc(s_rstd, 1)

        def relative(eng, e, done):
            if e == 0:
                eng.wait_ge(s_wlast, 16)
            eng.wait_ge(s_wb[e], 16)
            r = e % RAW
            eng.tensor_tensor(raw[:, r, 0, :], raw[:, r, 0, :], wlast[:, e, :], ALU.subtract)
            eng.tensor_tensor(raw[0:P - 1, r, 1, :], raw[0:P - 1, r, 1, :], wlast[0:P - 1, e, :],
                              ALU.subtract).then_inc(done, 1)

        @block.gpsimd
        def _(pool):
            pool.memset(kpad[:, L:L + P], 0.0).then_inc(s_const, 1)
            pool.memset(ident[:, :], 0.0).then_inc(s_zero, 1)
            pool.wait_ge(s_zero, 1)
            pool.affine_select(out=ident[:, :], in_=ident[:, :], compare_op=ALU.not_equal, fill=1.0, base=0,
                               pattern=[[-1, P]], channel_multiplier=1).then_inc(s_ident, 1)
            pool.memset(neghalf[:, :], -0.5).then_inc(s_zero, 1)
            pool.iota(eids[:, :], pattern=[[1, E]], base=0, channel_multiplier=0,
                      allow_small_or_imprecise_dtypes=True).then_inc(s_const, 1)
            pool.wait_ge(s_zero, 2)
            for n in range(2 * H):
                if not by_vector(n):
                    products(pool, n, s_kv)
                if n == 1:
                    inverse_std(pool, 0)
                if n == 11:
                    inverse_std(pool, 1)
                if n == 13:
                    pool.wait_ge(s_rb, 16)
                    pool.tensor_tensor(rw[:, 0], rw[:, 0], rwlast[:, :], ALU.subtract)
                    pool.tensor_tensor(rw[0:P - 1, 1], rw[0:P - 1, 1], rwlast[0:P - 1, :],
                                       ALU.subtract).then_inc(s_rrel, 1)
                if n in WREL:
                    relative(pool, WREL.index(n), s_wrel)
                if n == ZTS[0] - 1:
                    pool.wait_ge(s_qTp, LOADS)
                    pool.memset(qv[:, :, L - 1:L], 1.0).then_inc(s_one, 1)
                    inverse_std(pool, 2)
            for e in range(len(WREL), E):
                relative(pool, e, s_wrel)
            inverse_std(pool, 3)

            for b in range(B):
                if b == 0:
                    pool.wait_ge(s_half, 3)
                pool.wait_ge(s_z, b + 1)
                pool.tensor_tensor(xv[:, b, :], xv[:, b, :], obias[:, :], ALU.add).then_inc(s_xb, 1)

        @block.scalar
        def _(act):
            act.preload_act_table(ACT.Gelu_apprx_tanh)
            for i in range(2):
                load(act, cv, ctx_in, s_ctx, i)
            for i in range(2):
                load(act, xv, x, s_x, i)
            act.dma_start(gains[:, 0:1], everywhere(g_xattn, 0, 1)).then_inc(s_gin, 16)
            act.dma_start(gains[:, 1:2], everywhere(g_ffn, 0, 1)).then_inc(s_gin, 16)

            def evacuate(dst, banks, ready, done, i):
                act.wait_ge(ready, i + 1)
                g, k = divmod(i, BG // BL)
                act.activation(dst[:, g, :, BL * k:BL * (k + 1), :].rearrange("p c b n -> p c (b n)"),
                               banks[i % 2][:, :].rearrange("p (c n) -> p c n", c=C), ACT.Copy).then_inc(done, 1)

            def split_weights(e):
                act.wait_ge(s_wrel, e + 1)
                act.activation(w_hi[:, :, e, :], raw[:, e % RAW], ACT.Copy).then_inc(s_whi, 1)

            def z_high(b):
                act.wait_ge(s_zTp, b + 1)
                act.activation(zT_hi[:, b].rearrange("p c n -> p (c n)"), zbanks[b % 2][:, 0:L], ACT.Copy).then_inc(s_zhi, 1)

            def route(g):
                act.wait_ge(s_lgT, g + 1)
                act.activation(lgT_sb[:, :], red[0][0:E, :], ACT.Copy).then_inc(s_lgTe, 1)

            def route_columns(g):
                act.wait_ge(s_lgp, g + 1)
                if g:
                    act.wait_ge(s_gates, g)
                act.activation(lg[:, :], red[1][:, 0:BG * E], ACT.Copy).then_inc(s_lg, 1)

            def route_gap(g):
                act.wait_ge(s_gap, g + 1)
                act.activation(tgap[:, :], gap[:, :], ACT.Tanh, scale=0.5).then_inc(s_tgap, 1)

            def activate(n):
                act.wait_ge(s_exp, n + 1)
                if n >= GB:
                    act.wait_ge(s_mix, 2 * (n - GB + 1))
                act.activation(gelu[:, n % GB].rearrange("p e n -> p (e n)"), ring[n % RING][:, :],
                               ACT.Gelu_apprx_tanh).then_inc(s_gelu, 1)

            def mixed(b):
                act.wait_ge(s_mixp, b + 1)
                if b:
                    act.wait_ge(s_proj, b)
                act.activation(mixT_t[:, :], obank[:, 0:C * P], ACT.Copy).then_inc(s_mixT, 1)

            for i in range(2):
                evacuate(ctxT, red, s_cT, s_cTe, i)
            act.wait_ge(s_gin, 32)
            act.activation(tgains[:, :], gains[:, :], ACT.Tanh).then_inc(s_tg, 1)
            for i in range(2):
                evacuate(qT, (zbank, obank), s_qTp, s_qTe, i)
            for i in range(2, LOADS):
                evacuate(ctxT, red, s_cT, s_cTe, i)
            for i in range(2, LOADS):
                evacuate(qT, (zbank, obank), s_qTp, s_qTe, i)
            for e in range(len(WREL)):
                split_weights(e)
            for b in range(BG):
                z_high(b)
            route(0)
            route_columns(0)
            route_gap(0)
            for j, (b, k) in enumerate(BLOCKS):
                activate(j)
                if len(WREL) + j < E:
                    split_weights(len(WREL) + j)
                if j in LATE_ZTS:
                    z_high(BG + LATE_ZTS.index(j))
                if j == LATE_ZTS[-1] + 1:
                    route(1)
                if j == LATE_ZTS[-1] + 2:
                    route_columns(1)
                if j == LATE_ZTS[-1] + 3:
                    route_gap(1)
                if j in MIXED:
                    mixed(MIXED.index(j))
            mixed(B - 1)

        @block.tensor
        def _(pe):
            pe.wait_ge(s_ident, 1)

            def transposed(src, banks, produced, i):
                for c in range(C):
                    for b in range(BL):
                        last = pe.transpose(banks[i % 2][:, P * (BL * c + b):P * (BL * c + b + 1)],
                                            src[:, BL * i + b, P * c:P * (c + 1)], ident[:, :])
                last.then_inc(produced, 1)

            def context(i):
                pe.wait_ge(s_ctx[i], 16)
                if i >= 2:
                    pe.wait_ge(s_cTe, i - 1)
                transposed(cv, red, s_cT, i)

            def queries(i):
                pe.wait_ge(s_q, BL * (i + 1))
                if i >= 2:
                    pe.wait_ge(s_qTe, i - 1)
                transposed(qv, (zbank, obank), s_qTp, i)

            def ring_free(n):
                last = n - RING
                if last >= 2 * H:
                    pe.wait_ge(s_gelu, last - 2 * H + 1)
                elif last >= 0:
                    pe.wait_ge(s_zq, last + 1)

            def convolve(n):
                g, h = divmod(n, H)
                for i, (first, _) in enumerate(TOEP):
                    if n == first:
                        pe.wait_ge(s_toep[i], 16)
                if by_vector(n):
                    pe.wait_ge(s_kvd, n // DVE_EVERY + 1)
                else:
                    pe.wait_ge(s_kv, n - n // DVE_EVERY)
                ring_free(n)
                half = BG * NP
                y = ring[n % RING]
                src = kv[:, n % SLOTS].rearrange("p (c b) n -> p c (b n)", c=C)
                within, before = toep[:, h, P:2 * P], toep[:, h, 0:P]
                pe.matmul(y[:, 0:half], within, src[:, 0], start=True, stop=True)
                pe.matmul(y[:, half:2 * half], before, src[:, 0], start=True, stop=False)
                pe.matmul(y[:, half:2 * half], within, src[:, 1], start=False, stop=True).then_inc(s_conv, 1)

            def sum_channels(b):
                g = b // BG
                if b % BG == 0:
                    pe.wait_ge(s_zq, (g + 1) * H)
                if b >= 2:
                    pe.wait_ge(s_x1, b - 1)
                if b == BG:
                    pe.wait_ge(s_lgTe, 1)
                if b == BG + 1:
                    pe.wait_ge(s_lg, 1)
                for c in range(C):
                    for i in range(HD):
                        last = pe.matmul(red[b % 2][:, P * c:P * (c + 1)], zq[:, g, BG * c + b % BG, i, :], ident[:, :],
                                         is_transpose=True, start=(i == 0), stop=(i == HD - 1))
                last.then_inc(s_sum, 1)

            def z_transposed(b):
                pe.wait_ge(s_z, b + 1)
                if b >= 2:
                    pe.wait_ge(s_zlo, b - 1)
                for c in range(C):
                    last = pe.transpose(zbanks[b % 2][:, P * c:P * (c + 1)], qv[:, b, P * c:P * (c + 1)], ident[:, :])
                last.then_inc(s_zTp, 1)

            def route_logits(g):
                pe.wait_ge(s_rhl, 2)
                pe.wait_ge(s_zlo, BG * (g + 1))
                pe.wait_ge(s_x1, BG * (g + 1))
                own = slice(BG * g, BG * (g + 1))
                for c in range(C):
                    for n, (w, z) in enumerate(((rw_hi, zT_hi), (rw_hi, zT_lo), (rw_lo, zT_hi))):
                        last = pe.matmul(red[0][0:E, :], w[:, E * c:E * (c + 1)], z[:, own, c, :],
                                         start=(c == 0 and n == 0), stop=(c == C - 1 and n == 2))
                last.then_inc(s_lgT, 1)

            def route_rows(g):
                pe.wait_ge(s_lgTe, g + 1)
                for b in range(BG):
                    last = pe.transpose(red[1][:, E * b:E * (b + 1)], lgT_sb[:, P * b:P * (b + 1)], ident[0:E, 0:E])
                last.then_inc(s_lgp, 1)

            def experts(n, b, k):
                ring_free(2 * H + n)
                h = ring[n % RING]
                if b == 0:
                    pe.wait_ge(s_wlo, 2 * k + 2)
                for c in range(C):
                    hi, lo = zT_hi[:, b, c, :], zT_lo[:, b, c, :]
                    whi = w_hi[:, c, 2 * k:2 * k + 2, :].rearrange("p e n -> p (e n)")
                    wlo = w_lo[:, c, 2 * k:2 * k + 2, :].rearrange("p e n -> p (e n)")
                    pe.matmul(h[:, :], hi, whi, start=(c == 0), stop=False)
                    pe.matmul(h[:, :], hi, wlo, start=False, stop=False)
                    last = pe.matmul(h[:, :], lo, whi, start=False, stop=(c == C - 1))
                last.then_inc(s_exp, 1)

            def mix_transposed(b):
                pe.wait_ge(s_mix, added(b, EP - 1))
                if b:
                    pe.wait_ge(s_mixT, b)
                else:
                    pe.wait_ge(s_qTe, LOADS)
                for c in range(C):
                    last = pe.transpose(obank[:, P * c:P * (c + 1)], mix[:, b % BG, P * c:P * (c + 1)], ident[:, :])
                last.then_inc(s_mixp, 1)

            def project(b):
                if b == 0:
                    pe.wait_ge(s_ow, 16)
                if b:
                    pe.wait_ge(s_y, b)
                pe.wait_ge(s_mixT, b + 1)
                for c in range(C):
                    last = pe.matmul(zbank[:, 0:L], mixT[:, c, :], ow[:, c, :], start=(c == 0), stop=(c == C - 1))
                last.then_inc(s_proj, 1)

            for i in range(2):
                context(i)
            for n in range(2 * H):
                convolve(n)
                if n == 1:
                    queries(0)
                    queries(1)
                if n == 4:
                    context(2)
                    context(3)
                if n == 12:
                    queries(2)
                    queries(3)
                if n in SUMS:
                    sum_channels(SUMS.index(n))
                if n in ZTS:
                    z_transposed(ZTS.index(n))
                if n == ZTS[-1] + 1:
                    route_logits(0)
                if n == ZTS[-1] + 2:
                    route_rows(0)
            for j, (b, k) in enumerate(BLOCKS):
                experts(j, b, k)
                if j in LATE_SUMS:
                    sum_channels(BG + LATE_SUMS.index(j))
                if j in LATE_ZTS:
                    z_transposed(BG + LATE_ZTS.index(j))
                if j == LATE_ZTS[-1] + 1:
                    route_logits(1)
                if j == LATE_ZTS[-1] + 2:
                    route_rows(1)
                if j - 1 in MIXED:
                    project(MIXED.index(j - 1))
                if j in MIXED:
                    mix_transposed(MIXED.index(j))
            mix_transposed(B - 1)
            project(B - 1)

        @block.vector
        def _(dve):
            def statistics(b, n):
                dve.bn_stats(stats[:, 6 * b:6 * (b + 1)], xv[:, b, :]).then_inc(s_st, 1)
                dve.wait_ge(s_st, n + 1)
                dve.bn_aggr(mvv[:, n, :], stats[:, 6 * b:6 * (b + 1)]).then_inc(s_mv, 1)

            def add_eps(n):
                dve.wait_ge(s_mv, BG * (n + 1))
                dve.tensor_scalar(vareps[:, BG * n:BG * (n + 1)], mvv[:, BG * n:BG * (n + 1), 1], EPS, None,
                                  ALU.add).then_inc(s_ve, 1)

            def norm_x(g):
                for b in range(BG * g, BG * (g + 1)):
                    if b % BL == 0:
                        dve.wait_ge(s_x[b // BL], 16)
                    statistics(b, b)
                add_eps(g)

            def queries(g):
                own = slice(BG * g, BG * (g + 1))
                dve.wait_ge(s_rstd, g + 1)
                dve.wait_ge(s_tg, 1)
                dve.tensor_scalar(qscale[:, own], rstd[:, own], tgains[:, 0:1], None, ALU.mult).then_inc(s_qs, 1)
                dve.wait_ge(s_qs, g + 1)
                for b in range(BG * g, BG * (g + 1)):
                    dve.tensor_scalar(backwards(q_t, B * L, b * L), xv[:, b, :].rearrange("p (c n) -> p c n", c=C),
                                      mvv[:, b, 0:1], qscale[:, b:b + 1], ALU.subtract, ALU.mult).then_inc(s_q, 1)

            def query_products(n):
                g, h = divmod(n, H)
                if h == 0:
                    dve.wait_ge(s_qTe, (g + 1) * (BG // BL))
                dve.wait_ge(s_conv, n + 1)
                y = ring[n % RING][:, 0:CB * NP].rearrange("p (a n) -> p a n", a=CB)
                rows_lo = y[:, :, 0:NPU].rearrange("p a (i j) -> p a i j", i=HB)
                rows_hi = y[:, :, NPU:NP].rearrange("p a (i j) -> p a i j", i=HB)
                q = qTm[:, g, :, HD * h:HD * (h + 1)]
                dst = zq[:, g, :, :, HD * h:HD * (h + 1)]
                dve.tensor_tensor(dst[:, :, 0:HB, :], rows_lo, q[:, :, 0:HB].unsqueeze(3).to_broadcast([P, CB, HB, HD]),
                                  ALU.mult)
                q_hi = q[:, :, HB:HD].unsqueeze(3).to_broadcast([P, CB, HB, HB])
                dve.tensor_tensor(dst[:, :, HB:HD, HB:HD], rows_hi, q_hi, ALU.mult)
                dve.tensor_tensor(dst[:, :, HB:HD, 0:HB], rows_lo[:, :, :, HB:HD].rearrange("p a i j -> p a j i"), q_hi,
                                  ALU.mult).then_inc(s_zq, 1)

            def residual(b):
                dve.wait_ge(s_sum, b + 1)
                row = xv[:, b, :].rearrange("p (c n) -> p c n", c=C)
                dve.tensor_tensor(row, backwards(red[b % 2], 512, 0), row, ALU.add).then_inc(s_x1, 1)
                dve.wait_ge(s_x1, b + 1)
                statistics(b, B + b)

            def normalise(b):
                if b % BG == 0:
                    dve.wait_ge(s_rstd, 3 + b // BG)
                    dve.wait_ge(s_one, 1)
                dve.tensor_scalar(qv[:, b, 0:L - 1], xv[:, b, 0:L - 1], mvv[:, B + b, 0:1], rstd[:, B + b:B + b + 1],
                                  ALU.subtract, ALU.mult).then_inc(s_z, 1)

            def z_low(b):
                dve.wait_ge(s_zhi, b + 1)
                dve.tensor_tensor(zT_lo[:, b].rearrange("p c n -> p (c n)"), zbanks[b % 2][:, 0:L],
                                  zT_hi[:, b].rearrange("p c n -> p (c n)").bitcast(F32), ALU.subtract).then_inc(s_zlo, 1)

            def weights_low(e):
                dve.wait_ge(s_whi, e + 1)
                dve.tensor_tensor(w_lo[:, :, e, :], raw[:, e % RAW], w_hi[:, :, e, :].bitcast(F32),
                                  ALU.subtract).then_inc(s_wlo, 1)

            def router_split():
                dve.wait_ge(s_rrel, 1)
                dve.tensor_copy(rw_hi[:, :], rw_t[:, :]).then_inc(s_rhl, 1)
                dve.wait_ge(s_rhl, 1)
                dve.tensor_tensor(rw_lo[:, :], rw_t[:, :], rw_hi[:, :].bitcast(F32), ALU.subtract).then_inc(s_rhl, 1)

            def choose(g):
                dve.wait_ge(s_lg, g + 1)
                for b in range(BG):
                    dve.max(topv[:, b, :], lgv[:, b, :]).then_inc(s_max, 1)
                dve.wait_ge(s_max, BG * (g + 1))
                if g:
                    dve.wait_ge(s_tgap, g)
                dve.tensor_tensor(gap[:, :], topv[:, :, 0], topv[:, :, 1], ALU.subtract).then_inc(s_gap, 1)
                for b in range(BG):
                    last = dve.max_index(topiv[:, b, :], topv[:, b, :], lgv[:, b, :])
                last.then_inc(s_idx, 1)
                dve.wait_ge(s_idx, 2 * g + 1)
                dve.tensor_copy(topfv, topiv[:, :, 0:2]).then_inc(s_idx, 1)

            def weigh(g):
                dve.wait_ge(s_tgap, g + 1)
                dve.wait_ge(s_half, 2)
                dve.tensor_scalar(gate2[:, 0:BG], tgap[:, :], halfg[:, 0:1], halfg[:, 0:1], ALU.mult, ALU.add).then_inc(s_g, 1)
                dve.tensor_scalar(gate2[:, BG:2 * BG], tgap[:, :], halfg[:, 1:2], halfg[:, 0:1], ALU.mult,
                                  ALU.add).then_inc(s_g, 1)
                dve.wait_ge(s_idx, 2 * g + 2)
                for k in range(2):
                    dve.tensor_tensor(hitv[:, k], eids[:, :].unsqueeze(1).to_broadcast([P, BG, E]),
                                      topfv[:, :, k:k + 1].to_broadcast([P, BG, E]), ALU.is_equal).then_inc(s_hit, 1)
                dve.wait_ge(s_g, 2 * g + 2)
                dve.wait_ge(s_hit, 4 * g + 2)
                for k in range(2):
                    dve.tensor_tensor(hitv[:, k], hitv[:, k],
                                      gate2[:, BG * k:BG * (k + 1)].unsqueeze(2).to_broadcast([P, BG, E]),
                                      ALU.mult).then_inc(s_hit, 1)
                dve.wait_ge(s_hit, 4 * g + 4)
                dve.tensor_tensor(gates[:, BG * g:BG * (g + 1), :], hitv[:, 0], hitv[:, 1], ALU.add).then_inc(s_gates, 1)

            def accumulate(n, b, k):
                dve.wait_ge(s_gelu, n + 1)
                if k == 0 and b % BG == 0:
                    dve.wait_ge(s_gates, b // BG + 1)
                if k == 0 and b >= BG:
                    dve.wait_ge(s_mixp, b - BG + 1)
                acc = mix[:, b % BG, :]
                for e in range(2):
                    gate = gates[:, b, 2 * k + e:2 * k + e + 1]
                    if k == 0 and e == 0:
                        dve.tensor_scalar(acc, gelu[:, n % GB, e, :], gate, None, ALU.mult).then_inc(s_mix, 1)
                    else:
                        dve.wait_ge(s_mix, 2 * n + 1 if e else added(b, k - 1))
                        dve.scalar_tensor_tensor(out=acc, in0=gelu[:, n % GB, e, :], scalar=gate, in1=acc, op0=ALU.mult,
                                                 op1=ALU.add).then_inc(s_mix, 1)

            def finish(b):
                dve.wait_ge(s_proj, b + 1)
                dve.wait_ge(s_xb, b + 1)
                dve.tensor_tensor(xv[:, b, :], zbank[:, 0:L], xv[:, b, :], ALU.add).then_inc(s_y, 1)

            dve.wait_ge(s_kin, 32)
            dve.tensor_copy(kpad[:, 0:L - 1], bass.AP(mix_t, L - 1, [[BG * L, H], [-1, L - 1]]))
            dve.tensor_tensor(kpad[:, L - 1:L], taps[:, 0:1], dcol[:, :], ALU.add).then_inc(s_kd, 1)
            norm_x(0)
            products(dve, 0, s_kvd)
            queries(0)
            for n in range(2 * H):
                if n % DVE_EVERY == 1 and n + 3 < 2 * H:
                    products(dve, n + 3, s_kvd)
                query_products(n)
                if n == 5:
                    norm_x(1)
                if n == 10:
                    queries(1)
                if n == 14:
                    router_split()
                    dve.tensor_scalar(halfg[:, 0:1], tgains[:, 1:2], 0.5, None, ALU.mult).then_inc(s_half, 1)
                    dve.tensor_scalar(halfg[:, 1:2], tgains[:, 1:2], -0.5, None, ALU.mult).then_inc(s_half, 1)
                    dve.wait_ge(s_ob, 16)
                    dve.tensor_scalar(obias[:, :], obias[:, :], tgains[:, 1:2], None, ALU.mult).then_inc(s_half, 1)
                if n - 1 in SUMS:
                    residual(SUMS.index(n - 1))
                if n - 1 == SUMS[-1]:
                    add_eps(2)
                if n - 2 in WREL:
                    weights_low(WREL.index(n - 2))
                if n == ZTS[0] - 1:
                    for b in range(BG):
                        normalise(b)
                if n in ZTS:
                    z_low(ZTS.index(n))
            choose(0)
            weigh(0)
            for j, (b, k) in enumerate(BLOCKS):
                accumulate(j, b, k)
                if j in LATE_SUMS:
                    residual(BG + LATE_SUMS.index(j))
                if j == LATE_SUMS[-1]:
                    add_eps(3)
                if j % 2 == 0 and len(WREL) + j // 2 < E:
                    weights_low(len(WREL) + j // 2)
                if j == LATE_ZTS[0] - 1:
                    for s in range(BG, B):
                        normalise(s)
                if j in LATE_ZTS:
                    z_low(BG + LATE_ZTS.index(j))
                if j == LATE_ZTS[-1] + 2:
                    choose(1)
                if j == LATE_ZTS[-1] + 3:
                    weigh(1)
                if j - 1 in MIXED:
                    finish(MIXED.index(j - 1))
            finish(B - 1)


_INS = ["x", "ctx_2048", "g_xattn", "g_ffn", "L0_xattn_ssm_kernel", "L0_xattn_D", "L0_ffn_router_w", "L0_ffn_router_b",
        "L0_ffn_expert_w", "L0_ffn_expert_b", "L0_ffn_out_w", "L0_ffn_out_b"]


def kernel(**inputs):
    import numpy as _np
    import concourse.bacc as _bacc
    from concourse import mybir as _mybir
    from concourse.bass_utils import run_bass_kernel_spmd as _run

    nc = _bacc.Bacc("TRN2", target_bir_lowering=False, num_devices=1)
    arrays, args = {}, []
    for name in _INS:
        a = _np.ascontiguousarray(inputs[name])
        arrays[f"in_{name}"] = a
        args.append(nc.dram_tensor(f"in_{name}", a.shape, _mybir.dt.from_np(a.dtype), kind="ExternalInput").ap())
    shape = inputs["x"].shape
    args.append(nc.dram_tensor("out_0", shape, _mybir.dt.float32, kind="ExternalOutput").ap())
    flamingo_kernel(nc, *args)
    r = _run(nc, [arrays], core_ids=[0])
    return r.results[0]["out_0"]
```

```python
from contextlib import ExitStack

import concourse.bass as bass
from concourse import mybir

F32 = mybir.dt.float32
F32R = mybir.dt.float32r
U32 = mybir.dt.uint32
ALU = mybir.AluOpType
ACT = mybir.ActivationFunctionType

P = 128
HD = 8
HB = HD // 2
EPS = 1e-5
RING = 4
SLOTS = 8
RAW = 4
LOADS = 4
TOEP = ((0, 1), (1, 3), (4, 4), (8, 4), (12, 4))
BY_VECTOR = (0, 8, 13, 15, 18, 23, 24, 28, 30)
HALVED_BY_DVE, HALVED_BY_POOL = (1, 2, 3, 4, 5), (6, 7)
WARM_UP = (12, 1, 6, 1, 5, 5)

SUMS = (16, 18, 19, 21)
HALVES = (15, 15, 17)
ZTS = (27, 29, 30, 31)
ROUTER_SPLIT = 27
X_SCALES, X1_SCALES = 13, 27
ROUTER_REL = 15
WREL = (16, 18, 24, 29)

LATE_SUMS = (1, 2, 3, 4)
LATE_SPLIT = 5
LATE_ZTS = (10, 10, 12, 12)
LATE_ROUTE = 13
MIXED = (13, 15, 19, 21, 23, 25, 29)
PROJECTED = 5


def flamingo_kernel(nc, x, ctx_in, g_xattn, g_ffn, ssm_kernel, ssm_d, router_w, router_b, expert_w, expert_b,
                    out_w, out_b, out):
    B, S, L = x.shape
    H = ssm_kernel.shape[0]
    E = expert_w.shape[0]
    C = L // P
    G = 2
    BG = B // G
    CB = C * BG
    NP = HD * HD - HB * HB
    NPU = HB * HD
    BL = B // LOADS
    EP = E // 2
    assert S == P and H * HD == P and L == C * P and C == 2 and E * 4 * L * 4 <= 16 * 2048

    with ExitStack() as stack:
        def sb(name, shape, dt=F32):
            return stack.enter_context(nc.sbuf_tensor(name, shape, dt))

        def sem(name):
            return stack.enter_context(nc.semaphore(name))

        x_t = sb("x_t", [P, B * L])
        ctx_t = sb("ctx_t", [P, B * L])
        q_t = sb("q_t", [P, B * L])
        ctxT_t = sb("ctxT_t", [P, G * CB * P])
        qT_t = sb("qT_t", [P, G * CB * P])
        kv_t = sb("kv_t", [P, SLOTS * CB * NP])
        toep_t = sb("toep_t", [P, H * L])
        zq_t = sb("zq_t", [P, G * CB * HD * P])
        w_hi_t = sb("w_hi_t", [P, C * E * L], F32R)
        w_lo_t = sb("w_lo_t", [P, C * E * L], F32R)
        zT_hi_t = sb("zT_hi_t", [P, B * C * P], F32R)
        zT_lo_t = sb("zT_lo_t", [P, B * C * P], F32R)
        wlast_t = sb("wlast_t", [P, E * L])
        mix_t = sb("mix_t", [P, BG * L])
        mixT_hi_t = sb("mixT_hi_t", [P, 2 * C * P], F32R)
        mixT_lo_t = sb("mixT_lo_t", [P, 2 * C * P], F32R)
        ow_hi_t = sb("ow_hi_t", [P, C * L], F32R)
        ow_lo_t = sb("ow_lo_t", [P, C * L], F32R)
        ow_t = sb("ow_t", [P, C * L])
        obias = sb("obias", [P, L])
        rw_t = sb("rw_t", [P, C * E])
        rwlast = sb("rwlast", [P, E])
        rw_hi = sb("rw_hi", [P, C * E], F32R)
        rw_lo = sb("rw_lo", [P, C * E], F32R)
        ident = sb("ident", [P, P])
        dcol = sb("dcol", [H, 1])
        gains = sb("gains", [P, 2])
        tgains = sb("tgains", [P, 2])
        halfg = sb("halfg", [P, 2])
        neghalf = sb("neghalf", [P, BG])
        stats = sb("stats", [P, BG * 6])
        mv = sb("mv", [P, BG * 2])
        negmean = sb("negmean", [P, 2 * B])
        sumsq = sb("sumsq", [P, 2 * B])
        vareps = sb("vareps", [P, 2 * B])
        rstd = sb("rstd", [P, 2 * B])
        shift = sb("shift", [P, 2 * B])
        qscale = sb("qscale", [P, B])
        junk = sb("junk", [P, 2 * L])
        lg = sb("lg", [P, BG * E])
        top = sb("top", [P, BG * 8])
        topi = sb("topi", [P, BG * 8], U32)
        topf = sb("topf", [P, BG * 2])
        gap = sb("gap", [P, BG])
        tgap = sb("tgap", [P, BG])
        gate2 = sb("gate2", [P, 2 * BG])
        eids = sb("eids", [P, E])
        hit = sb("hit", [P, 2 * BG * E])
        gates_t = sb("gates_t", [P, B * E])
        scratch = nc.dram_tensor("kpad_dram", [H, L + P], F32, kind="Internal").ap()

        xv = x_t[:, :].rearrange("p (b l) -> p b l", b=B)
        cv = ctx_t[:, :].rearrange("p (b l) -> p b l", b=B)
        qv = q_t[:, :].rearrange("p (b l) -> p b l", b=B)
        ctxT = ctxT_t[:, :].rearrange("p (g c b n) -> p g c b n", g=G, c=C, b=BG)
        qT = qT_t[:, :].rearrange("p (g c b n) -> p g c b n", g=G, c=C, b=BG)
        ctxTm = ctxT_t[:, :].rearrange("p (g a n) -> p g a n", g=G, a=CB)
        qTm = qT_t[:, :].rearrange("p (g a n) -> p g a n", g=G, a=CB)
        kv = kv_t[:, :].rearrange("p (s a n) -> p s a n", s=SLOTS, a=CB)
        toep = toep_t[:, :].rearrange("p (h l) -> p h l", h=H)
        zq = zq_t[:, :].rearrange("p (g a i n) -> p g a i n", g=G, a=CB, i=HD)
        w_hi = w_hi_t[:, :].rearrange("p (c e n) -> p c e n", c=C, e=E)
        w_lo = w_lo_t[:, :].rearrange("p (c e n) -> p c e n", c=C, e=E)
        zT_hi = zT_hi_t[:, :].rearrange("p (b c n) -> p b c n", b=B, c=C)
        zT_lo = zT_lo_t[:, :].rearrange("p (b c n) -> p b c n", b=B, c=C)
        raw = ctx_t[:, :].rearrange("p (r c n) -> p r c n", r=RAW, c=C)
        wlast = wlast_t[:, :].rearrange("p (e n) -> p e n", e=E)
        mix = mix_t[:, :].rearrange("p (s n) -> p s n", s=BG)
        taps, kpad = mix_t[0:H, 0:L], mix_t[0:H, L:2 * L + P]
        mixT_hi = mixT_hi_t[:, :].rearrange("p (s n) -> p s n", s=2)
        mixT_lo = mixT_lo_t[:, :].rearrange("p (s n) -> p s n", s=2)
        ow_hi = ow_hi_t[:, :].rearrange("p (c n) -> p c n", c=C)
        ow_lo = ow_lo_t[:, :].rearrange("p (c n) -> p c n", c=C)
        ow = ow_t[:, :].rearrange("p (c n) -> p c n", c=C)
        last_mixT = zq_t[:, 0:C * P]
        lgT_sb = qT_t[0:E, 0:BG * P]
        rw = rw_t[:, :].rearrange("p (c n) -> p c n", c=C)
        lgv = lg[:, :].rearrange("p (b e) -> p b e", b=BG)
        topv = top[:, :].rearrange("p (b e) -> p b e", b=BG)
        topiv = topi[:, :].rearrange("p (b e) -> p b e", b=BG)
        topfv = topf[:, :].rearrange("p (b k) -> p b k", b=BG)
        hitv = hit[:, :].rearrange("p (k b e) -> p k b e", k=2, b=BG)
        gates = gates_t[:, :].rearrange("p (b e) -> p b e", b=B)
        mvv = mv[:, :].rearrange("p (b k) -> p b k", k=2)

        ring = [stack.enter_context(nc.psum_tensor(f"ring{i}", [P, 512], F32)) for i in range(RING)]
        red = [stack.enter_context(nc.psum_tensor(f"red{i}", [P, 512], F32)) for i in range(2)]
        zbank = stack.enter_context(nc.psum_tensor("zbank", [P, 512], F32))
        obank = stack.enter_context(nc.psum_tensor("obank", [P, 512], F32))

        zbanks = (zbank, red[1])
        taps_in = sem("taps_in")
        scratch_written = sem("scratch_written")
        gains_in = sem("gains_in")
        context_in = [sem(f"context_in{i}") for i in range(LOADS)]
        x_in = [sem(f"x_in{i}") for i in range(LOADS)]
        toeplitz_in = [sem(f"toeplitz_in{i}") for i in range(len(TOEP))]
        router_in = sem("router_in")
        router_bias_in = sem("router_bias_in")
        last_rows_in = sem("last_rows_in")
        weights_in = [sem(f"weights_in{i}") for i in range(E)]
        bias_in = [sem(f"bias_in{i}") for i in range(E)]
        out_weights_in = sem("out_weights_in")
        out_bias_in = sem("out_bias_in")
        results_out = sem("results_out")
        zeroed = sem("zeroed")
        constants_ready = sem("constants_ready")
        identity_ready = sem("identity_ready")
        pool_products_ready = sem("pool_products_ready")
        pool_halved = sem("pool_halved")
        inverse_std_ready = sem("inverse_std_ready")
        variances_ready = sem("variances_ready")
        late_query_scales_ready = sem("late_query_scales_ready")
        shifts_ready = sem("shifts_ready")
        router_relative = sem("router_relative")
        weights_relative = sem("weights_relative")
        weights_low_ready = sem("weights_low_ready")
        ones_ready = sem("ones_ready")
        bias_added = sem("bias_added")
        context_transposed = sem("context_transposed")
        queries_transposed = sem("queries_transposed")
        convolved = sem("convolved")
        summed = sem("summed")
        zT_ready = sem("zT_ready")
        logits_ready = sem("logits_ready")
        logit_rows_ready = sem("logit_rows_ready")
        experts_ready = sem("experts_ready")
        mixture_transposed = sem("mixture_transposed")
        projected = sem("projected")
        tanh_ready = sem("tanh_ready")
        context_evacuated = sem("context_evacuated")
        act_queries_evacuated = sem("act_queries_evacuated")
        means_ready = sem("means_ready")
        squares_ready = sem("squares_ready")
        late_queries_ready = sem("late_queries_ready")
        z_ready = sem("z_ready")
        z_high_ready = sem("z_high_ready")
        weights_high_ready = sem("weights_high_ready")
        out_weights_high_ready = sem("out_weights_high_ready")
        logits_evacuated = sem("logits_evacuated")
        logit_rows_evacuated = sem("logit_rows_evacuated")
        gap_tanh_ready = sem("gap_tanh_ready")
        gelu_ready = sem("gelu_ready")
        mixture_high_ready = sem("mixture_high_ready")
        taps_reversed = sem("taps_reversed")
        dve_products_ready = sem("dve_products_ready")
        dve_halved = sem("dve_halved")
        row_stats_ready = sem("row_stats_ready")
        moments_ready = sem("moments_ready")
        first_variances_ready = sem("first_variances_ready")
        first_query_scales_ready = sem("first_query_scales_ready")
        first_queries_ready = sem("first_queries_ready")
        dve_queries_evacuated = sem("dve_queries_evacuated")
        read_out = sem("read_out")
        x1_ready = sem("x1_ready")
        z_low_ready = sem("z_low_ready")
        router_split_ready = sem("router_split_ready")
        gain_terms_ready = sem("gain_terms_ready")
        tops_ready = sem("tops_ready")
        gap_ready = sem("gap_ready")
        indices_ready = sem("indices_ready")
        gate_pair_ready = sem("gate_pair_ready")
        hits_ready = sem("hits_ready")
        gates_ready = sem("gates_ready")
        mixed_in = sem("mixed_in")
        out_weights_low_ready = sem("out_weights_low_ready")
        mixture_low_ready = sem("mixture_low_ready")
        y_ready = sem("y_ready")

        block = stack.enter_context(nc.Block())

        BLOCKS = [(b, k) for k in range(EP) for b in range(BG)] + [(b, k) for b in range(BG, B) for k in range(EP)]

        def due(schedule, n):
            return [i for i, at in enumerate(schedule) if at == n]

        def added(b, k):
            return 2 * BLOCKS.index((b, k)) + 2

        def rows(src, b0, n):
            return src[b0:b0 + n].rearrange("b s l -> s b l")

        def load(eng, dst, src, done, i):
            eng.dma_start(dst[:, BL * i:BL * (i + 1), :], rows(src, BL * i, BL)).then_inc(done[i], 16)

        def everywhere(src, offset, n):
            return bass.AP(src.tensor, offset, [[0, P], [1, n]])

        def backwards(tensor, width, offset):
            return bass.AP(tensor, offset + P - 1, [[width, P], [P, C], [-1, P]])

        def raw_weights(sp, e):
            if e >= RAW:
                sp.wait_ge(weights_high_ready, e - RAW + 1)
                sp.wait_ge(weights_low_ready, e - RAW + 1)
            sp.dma_start(raw[:, e % RAW], expert_w[e].rearrange("(c p) n -> p c n", c=C)).then_inc(weights_in[e], 16)

        def raw_bias(sp, e):
            sp.wait_ge(weights_in[e], 16)
            sp.dma_start(raw[P - 1:P, e % RAW, 1, :], expert_b[e:e + 1, :]).then_inc(bias_in[e], 16)

        @block.sync
        def _(sp):
            sp.dma_start(taps[:, :], ssm_kernel).then_inc(taps_in, 16)
            sp.dma_start(dcol[:, :], ssm_d.rearrange("(h a) -> h a", a=1)).then_inc(taps_in, 16)
            sp.wait_ge(taps_reversed, 1)
            sp.wait_ge(constants_ready, 1)
            sp.dma_start(scratch, kpad[:, :]).then_inc(scratch_written, 16)
            for i in range(2, LOADS):
                load(sp, cv, ctx_in, context_in, i)
            sp.wait_ge(scratch_written, 16)
            for i, (h, n) in enumerate(TOEP):
                src = bass.AP(scratch.tensor, h * (P + L), [[1, P], [P + L, n], [1, L]])
                sp.dma_start(toep[:, h:h + n, :], src).then_inc(toeplitz_in[i], 16)
            for i in range(2, LOADS):
                load(sp, xv, x, x_in, i)
            sp.dma_start(wlast, bass.AP(expert_w.tensor, (L - 1) * L,
                                        [[0, P], [L * L, E], [1, L]])).then_inc(last_rows_in, 16)
            sp.dma_start(rw, router_w.rearrange("(c p) n -> p c n", c=C)).then_inc(router_in, 16)
            sp.dma_start(rwlast[:, :], everywhere(router_w, (L - 1) * E, E)).then_inc(router_in, 16)
            sp.dma_start(obias[:, :], everywhere(out_b, 0, L)).then_inc(out_bias_in, 16)
            sp.dma_start(ow, out_w.rearrange("(c p) n -> p c n", c=C)).then_inc(out_weights_in, 16)
            sp.wait_ge(router_in, 32)
            sp.dma_start(rw_t[P - 1:P, E:2 * E], router_b.rearrange("(a n) -> a n", a=1)).then_inc(router_bias_in, 16)
            sp.wait_ge(context_transposed, B // BL)
            for e in range(RAW):
                raw_weights(sp, e)
            for e in range(RAW):
                raw_bias(sp, e)
            raw_weights(sp, RAW)
            for e in range(RAW + 1, E):
                raw_weights(sp, e)
                raw_bias(sp, e - 1)
            raw_bias(sp, E - 1)
            for b in range(B):
                sp.wait_ge(y_ready, b + 1)
                sp.dma_start(out[b], xv[:, b, :]).then_inc(results_out, 16)
            sp.wait_ge(results_out, 16 * B)

        def by_vector(n):
            return n in BY_VECTOR

        def products(eng, n, done):
            g, h = divmod(n, H)
            if n % H < 2:
                eng.wait_ge(context_evacuated, (g + 1) * (BG // BL))
            if n >= SLOTS:
                eng.wait_ge(convolved, n - SLOTS + 1)
            head = ctxTm[:, g, :, HD * h:HD * (h + 1)]
            lower = head[:, :, 0:HB]
            upper = head[:, :, HB:HD]
            dst = kv[:, n % SLOTS]
            eng.tensor_tensor(dst[:, :, 0:NPU].rearrange("p a (i j) -> p a i j", i=HB),
                              lower.unsqueeze(3).to_broadcast([P, CB, HB, HD]),
                              head.unsqueeze(2).to_broadcast([P, CB, HB, HD]), ALU.mult)
            eng.tensor_tensor(dst[:, :, NPU:NP].rearrange("p a (i j) -> p a i j", i=HB),
                              upper.unsqueeze(3).to_broadcast([P, CB, HB, HB]),
                              upper.unsqueeze(2).to_broadcast([P, CB, HB, HB]), ALU.mult).then_inc(done, 1)

        def halve_sum(eng, b, done):
            eng.wait_ge(read_out, (b // BG + 1) * H)
            terms = zq[:, b // BG, :, :, :].rearrange("p (c b) i n -> p c b (i n)", c=C)[:, :, b % BG, :]
            eng.tensor_tensor(terms[:, :, 0:HB * P], terms[:, :, 0:HB * P], terms[:, :, HB * P:HD * P],
                              ALU.add).then_inc(done, 1)

        @block.gpsimd
        def _(pool):
            def inverse_std(n):
                pool.tensor_tensor(rstd[:, BG * n:BG * (n + 1)], vareps[:, BG * n:BG * (n + 1)], neghalf[:, :],
                                   ALU.pow).then_inc(inverse_std_ready, 1)

            def scales(n):
                own = slice(BG * n, BG * (n + 1))
                pool.wait_ge(squares_ready, BG * n)
                pool.tensor_scalar(vareps[:, own], sumsq[:, own], 1.0 / L, EPS, ALU.mult,
                                   ALU.add).then_inc(variances_ready, 1)
                pool.wait_ge(variances_ready, n)
                inverse_std(n)
                pool.wait_ge(inverse_std_ready, n + 1)
                scale = rstd[:, own]
                if n == 1:
                    pool.wait_ge(tanh_ready, 1)
                    scale = qscale[:, own]
                    pool.tensor_scalar(scale, rstd[:, own], tgains[:, 0:1], None,
                                       ALU.mult).then_inc(late_query_scales_ready, 1)
                    pool.wait_ge(late_query_scales_ready, 1)
                pool.tensor_tensor(shift[:, own], negmean[:, own], scale, ALU.mult).then_inc(shifts_ready, 1)

            def relative(e):
                if e == 0:
                    pool.wait_ge(last_rows_in, 16)
                pool.wait_ge(bias_in[e], 16)
                r = e % RAW
                pool.tensor_tensor(raw[:, r, 0, :], raw[:, r, 0, :], wlast[:, e, :], ALU.subtract)
                pool.tensor_tensor(raw[0:P - 1, r, 1, :], raw[0:P - 1, r, 1, :], wlast[0:P - 1, e, :],
                                   ALU.subtract).then_inc(weights_relative, 1)

            def weights_low(e):
                pool.wait_ge(weights_high_ready, e + 1)
                pool.tensor_tensor(w_lo[:, :, e, :], raw[:, e % RAW], w_hi[:, :, e, :].bitcast(F32),
                                   ALU.subtract).then_inc(weights_low_ready, 1)

            pool.memset(kpad[:, L:L + P], 0.0).then_inc(constants_ready, 1)
            pool.memset(ident[:, :], 0.0).then_inc(zeroed, 1)
            pool.wait_ge(zeroed, 1)
            pool.affine_select(out=ident[:, :], in_=ident[:, :], compare_op=ALU.not_equal, fill=1.0, base=0,
                               pattern=[[-1, P]], channel_multiplier=1).then_inc(identity_ready, 1)
            pool.memset(neghalf[:, :], -0.5).then_inc(zeroed, 1)
            pool.iota(eids[:, :], pattern=[[1, E]], base=0, channel_multiplier=0,
                      allow_small_or_imprecise_dtypes=True).then_inc(constants_ready, 1)
            pool.wait_ge(zeroed, 2)
            for n in range(2 * H):
                if not by_vector(n):
                    products(pool, n, pool_products_ready)
                if n == 1:
                    pool.wait_ge(first_variances_ready, 1)
                    inverse_std(0)
                if n == X_SCALES:
                    scales(1)
                if n == ROUTER_REL:
                    pool.wait_ge(router_bias_in, 16)
                    pool.tensor_tensor(rw[:, 0], rw[:, 0], rwlast[:, :], ALU.subtract)
                    pool.tensor_tensor(rw[0:P - 1, 1], rw[0:P - 1, 1], rwlast[0:P - 1, :],
                                       ALU.subtract).then_inc(router_relative, 1)
                for i in due(WREL, n):
                    relative(i)
                for i in due(WREL, n - 2):
                    weights_low(i)
                if n == ZTS[0] - 1:
                    pool.wait_ge(queries_transposed, LOADS)
                    pool.memset(qv[:, :, L - 1:L], 1.0).then_inc(ones_ready, 1)
                if n == X1_SCALES:
                    scales(2)
            first = len(WREL)
            relative(first)
            relative(first + 1)
            halve_sum(pool, HALVED_BY_POOL[0], pool_halved)
            weights_low(first)
            halve_sum(pool, HALVED_BY_POOL[1], pool_halved)
            weights_low(first + 1)
            for e in range(first + 2, E):
                relative(e)
            scales(3)
            for e in range(first + 2, E):
                weights_low(e)

            for b in range(B):
                if b == 0:
                    pool.wait_ge(gain_terms_ready, 3)
                pool.wait_ge(z_ready, b + 1)
                pool.tensor_tensor(xv[:, b, :], xv[:, b, :], obias[:, :], ALU.add).then_inc(bias_added, 1)

        @block.scalar
        def _(act):
            act.preload_act_table(ACT.Gelu_apprx_tanh)
            for i in range(2):
                load(act, cv, ctx_in, context_in, i)
            for i in range(2):
                load(act, xv, x, x_in, i)
            act.dma_start(gains[:, 0:1], everywhere(g_xattn, 0, 1)).then_inc(gains_in, 16)
            act.dma_start(gains[:, 1:2], everywhere(g_ffn, 0, 1)).then_inc(gains_in, 16)

            def evacuate(dst, banks, ready, done, i):
                act.wait_ge(ready, i + 1)
                g, k = divmod(i, BG // BL)
                act.activation(dst[:, g, :, BL * k:BL * (k + 1), :].rearrange("p c b n -> p c (b n)"),
                               banks[i % 2][:, :].rearrange("p (c n) -> p c n", c=C), ACT.Copy).then_inc(done, 1)

            def statistics(n):
                b, calls = n % B, n - BG
                if n >= B:
                    act.wait_ge(x1_ready, b + 1)
                elif b % BL == 0:
                    act.wait_ge(x_in[b // BL], 16)
                act.activation(junk[:, 0:L], xv[:, b, :], ACT.Identity, scale=-1.0 / L,
                               accum_out=negmean[:, n:n + 1]).then_inc(means_ready, 1)
                act.wait_ge(means_ready, calls + 1)
                if calls:
                    act.wait_ge(squares_ready, calls)
                act.activation(junk[:, L:2 * L], xv[:, b, :], ACT.Square, bias=negmean[:, n:n + 1],
                               accum_out=sumsq[:, n:n + 1]).then_inc(squares_ready, 1)

            def queries(i):
                act.wait_ge(shifts_ready, 1)
                for b in range(BL * i, BL * (i + 1)):
                    act.activation(backwards(q_t, B * L, b * L), xv[:, b, :].rearrange("p (c n) -> p c n", c=C),
                                   ACT.Identity, scale=qscale[:, b:b + 1],
                                   bias=shift[:, b:b + 1]).then_inc(late_queries_ready, 1)

            def split_weights(e):
                act.wait_ge(weights_relative, e + 1)
                act.activation(w_hi[:, :, e, :], raw[:, e % RAW], ACT.Copy).then_inc(weights_high_ready, 1)

            def projection_high():
                act.wait_ge(out_weights_in, 16)
                act.activation(ow_hi_t[:, :], ow_t[:, :], ACT.Copy).then_inc(out_weights_high_ready, 1)

            def normalise(b):
                if b % BG == 0:
                    act.wait_ge(shifts_ready, 2 + b // BG)
                    act.wait_ge(ones_ready, 1)
                act.activation(qv[:, b, 0:L - 1], xv[:, b, 0:L - 1], ACT.Identity, scale=rstd[:, B + b:B + b + 1],
                               bias=shift[:, B + b:B + b + 1]).then_inc(z_ready, 1)

            def z_high(b):
                act.wait_ge(zT_ready, b + 1)
                act.activation(zT_hi[:, b].rearrange("p c n -> p (c n)"), zbanks[b % 2][:, 0:L],
                               ACT.Copy).then_inc(z_high_ready, 1)

            def route(g):
                act.wait_ge(logits_ready, g + 1)
                act.activation(lgT_sb[:, :], red[0][0:E, :], ACT.Copy).then_inc(logits_evacuated, 1)

            def route_columns(g):
                act.wait_ge(logit_rows_ready, g + 1)
                if g:
                    act.wait_ge(gates_ready, g)
                act.activation(lg[:, :], red[1][:, 0:BG * E], ACT.Copy).then_inc(logit_rows_evacuated, 1)

            def route_gap(g):
                act.wait_ge(gap_ready, g + 1)
                act.activation(tgap[:, :], gap[:, :], ACT.Tanh, scale=0.5).then_inc(gap_tanh_ready, 1)

            def activate(n):
                for e, m in ((0, 1), (1, 1)) if n == len(BLOCKS) - 1 else ((0, 2),):
                    act.wait_ge(experts_ready, n + e + 1)
                    y = ring[(n + e) % RING][:, 0:L * m]
                    act.activation(y, y, ACT.Gelu_apprx_tanh).then_inc(gelu_ready, 1)

            def mixed(b):
                act.wait_ge(mixture_transposed, b + 1)
                if b >= 2:
                    act.wait_ge(projected, b - 1)
                act.activation(mixT_hi[:, b % 2], obank[:, 0:C * P], ACT.Copy).then_inc(mixture_high_ready, 1)

            for i in range(2):
                evacuate(ctxT, red, context_transposed, context_evacuated, i)
            act.wait_ge(gains_in, 32)
            act.activation(tgains[:, :], gains[:, :], ACT.Tanh).then_inc(tanh_ready, 1)
            for i in range(2, LOADS):
                evacuate(ctxT, red, context_transposed, context_evacuated, i)
            evacuate(qT, (zbank, obank), queries_transposed, act_queries_evacuated, 0)
            for b in range(BG, B):
                statistics(b)
            for i in range(2, LOADS):
                queries(i)
            for i in range(2, LOADS):
                evacuate(qT, (zbank, obank), queries_transposed, act_queries_evacuated, i)
            split_weights(0)
            split_weights(1)
            statistics(B)
            statistics(B + 1)
            split_weights(2)
            statistics(B + 2)
            statistics(B + 3)
            normalise(0)
            normalise(1)
            for b in range(BG):
                z_high(b)
                if b + 2 < BG:
                    normalise(b + 2)
                if b == 1:
                    split_weights(3)
            projection_high()
            for j, (b, k) in enumerate(BLOCKS):
                activate(j)
                for i in due(LATE_SUMS[1:], j):
                    statistics(B + BG + i + 1)
                if j == LATE_SPLIT:
                    for e in range(len(WREL) + 2, E):
                        split_weights(e)
                if j == 0:
                    route(0)
                    split_weights(len(WREL))
                if j == 1:
                    split_weights(len(WREL) + 1)
                    route_columns(0)
                    statistics(B + BG)
                    route_gap(0)
                if j == LATE_ZTS[0] - 2:
                    normalise(BG)
                    normalise(BG + 1)
                if j == LATE_ZTS[0] - 1:
                    normalise(BG + 2)
                    normalise(BG + 3)
                for i in due(LATE_ZTS, j):
                    z_high(BG + i)
                if j == LATE_ROUTE:
                    route(1)
                if j == LATE_ROUTE + 1:
                    route_columns(1)
                if j == LATE_ROUTE + 2:
                    route_gap(1)
                for i in due(MIXED, j):
                    mixed(i)
            act.wait_ge(mixture_transposed, B)
            act.activation(last_mixT[:, 0:P], obank[:, 0:P], ACT.Copy).then_inc(mixture_high_ready, 1)

        @block.tensor
        def _(pe):
            pe.wait_ge(identity_ready, 1)

            def warm_up(n, bank):
                for _ in range(n):
                    pe.transpose(bank[:, 0:P], ident[:, :], ident[:, :])

            def transposed(src, banks, produced, i):
                for c in range(C):
                    for b in range(BL):
                        last = pe.transpose(banks[i % 2][:, P * (BL * c + b):P * (BL * c + b + 1)],
                                            src[:, BL * i + b, P * c:P * (c + 1)], ident[:, :])
                last.then_inc(produced, 1)

            def context(i):
                pe.wait_ge(context_in[i], 16)
                if i >= 2:
                    pe.wait_ge(context_evacuated, i - 1)
                transposed(cv, red, context_transposed, i)

            def queries(i):
                if i < 2:
                    pe.wait_ge(first_queries_ready, BL * (i + 1))
                else:
                    pe.wait_ge(late_queries_ready, BL * (i - 1))
                if i == 2:
                    pe.wait_ge(act_queries_evacuated, 1)
                if i == 3:
                    pe.wait_ge(dve_queries_evacuated, 1)
                transposed(qv, (zbank, obank), queries_transposed, i)

            def ring_free(n):
                last = n - RING
                if last >= 2 * H:
                    pe.wait_ge(mixed_in, 2 * (last - 2 * H + 1))
                elif last >= 0:
                    pe.wait_ge(read_out, last + 1)

            def convolve(n):
                g, h = divmod(n, H)
                for i, (first, _) in enumerate(TOEP):
                    if n == first:
                        pe.wait_ge(toeplitz_in[i], 16)
                if by_vector(n):
                    pe.wait_ge(dve_products_ready, BY_VECTOR.index(n) + 1)
                else:
                    pe.wait_ge(pool_products_ready, n + 1 - sum(by_vector(m) for m in range(n)))
                ring_free(n)
                half = BG * NP
                y = ring[n % RING]
                src = kv[:, n % SLOTS].rearrange("p (c b) n -> p c (b n)", c=C)
                within, before = toep[:, h, P:2 * P], toep[:, h, 0:P]
                pe.matmul(y[:, 0:half], within, src[:, 0], start=True, stop=True)
                pe.matmul(y[:, half:2 * half], before, src[:, 0], start=True, stop=False)
                pe.matmul(y[:, half:2 * half], within, src[:, 1], start=False, stop=True).then_inc(convolved, 1)

            def sum_channels(b):
                g = b // BG
                if b % BG == 0:
                    pe.wait_ge(read_out, (g + 1) * H)
                if b >= 2:
                    pe.wait_ge(x1_ready, b - 1)
                if b == BG:
                    pe.wait_ge(logits_evacuated, 1)
                if b == BG + 1:
                    pe.wait_ge(logit_rows_evacuated, 1)
                n = HD
                if b in HALVED_BY_DVE:
                    pe.wait_ge(dve_halved, HALVED_BY_DVE.index(b) + 1)
                    n = HB
                if b in HALVED_BY_POOL:
                    pe.wait_ge(pool_halved, HALVED_BY_POOL.index(b) + 1)
                    n = HB
                for c in range(C):
                    for i in range(n):
                        last = pe.matmul(red[b % 2][:, P * c:P * (c + 1)], zq[:, g, BG * c + b % BG, i, :], ident[:, :],
                                         is_transpose=True, start=(i == 0), stop=(i == n - 1))
                last.then_inc(summed, 1)

            def z_transposed(b):
                pe.wait_ge(z_ready, b + 1)
                if b >= 2:
                    pe.wait_ge(z_low_ready, b - 1)
                for c in range(C):
                    last = pe.transpose(zbanks[b % 2][:, P * c:P * (c + 1)], qv[:, b, P * c:P * (c + 1)], ident[:, :])
                last.then_inc(zT_ready, 1)

            def route_logits(g):
                pe.wait_ge(router_split_ready, 2)
                pe.wait_ge(z_low_ready, BG * (g + 1))
                pe.wait_ge(x1_ready, BG * (g + 1))
                own = slice(BG * g, BG * (g + 1))
                for c in range(C):
                    for n, (w, z) in enumerate(((rw_hi, zT_hi), (rw_hi, zT_lo), (rw_lo, zT_hi))):
                        last = pe.matmul(red[0][0:E, :], w[:, E * c:E * (c + 1)], z[:, own, c, :],
                                         start=(c == 0 and n == 0), stop=(c == C - 1 and n == 2))
                last.then_inc(logits_ready, 1)

            def route_rows(g):
                pe.wait_ge(logits_evacuated, g + 1)
                for b in range(BG):
                    last = pe.transpose(red[1][:, E * b:E * (b + 1)], lgT_sb[:, P * b:P * (b + 1)], ident[0:E, 0:E])
                last.then_inc(logit_rows_ready, 1)

            def experts(n, b, k):
                ring_free(2 * H + n)
                h = ring[n % RING]
                if b == 0:
                    pe.wait_ge(weights_low_ready, 2 * k + 2)
                for e, m in ((0, 1), (1, 1)) if n == len(BLOCKS) - 1 else ((0, 2),):
                    if e:
                        h = ring[(n + 1) % RING]
                        pe.wait_ge(mixed_in, 2 * (n + 2 - RING))
                    y = h[:, 0:L * m]
                    for c in range(C):
                        hi, lo = zT_hi[:, b, c, :], zT_lo[:, b, c, :]
                        whi = w_hi[:, c, 2 * k + e:2 * k + e + m, :].rearrange("p e n -> p (e n)")
                        wlo = w_lo[:, c, 2 * k + e:2 * k + e + m, :].rearrange("p e n -> p (e n)")
                        pe.matmul(y, hi, whi, start=(c == 0), stop=False)
                        pe.matmul(y, hi, wlo, start=False, stop=False)
                        last = pe.matmul(y, lo, whi, start=False, stop=(c == C - 1))
                    last.then_inc(experts_ready, 1)

            def mix_transposed(b):
                pe.wait_ge(mixed_in, added(b, EP - 1))
                if b:
                    pe.wait_ge(mixture_low_ready, b)
                else:
                    pe.wait_ge(act_queries_evacuated, LOADS - 1)
                for c in range(C):
                    last = pe.transpose(obank[:, P * c:P * (c + 1)], mix[:, b % BG, P * c:P * (c + 1)], ident[:, :])
                last.then_inc(mixture_transposed, 1)

            def last_mixture():
                pe.wait_ge(mixture_low_ready, B - 1)
                for c in range(C):
                    pe.wait_ge(mixed_in, 2 * len(BLOCKS) + c)
                    pe.transpose((obank, red[1])[c][:, 0:P], mix[:, (B - 1) % BG, P * c:P * (c + 1)],
                                 ident[:, :]).then_inc(mixture_transposed, 1)
                pe.wait_ge(y_ready, B - 1)
                pe.wait_ge(mixture_high_ready, B)
                pe.matmul(zbank[:, 0:L], last_mixT[:, 0:P], ow[:, 0, :], start=True, stop=False)
                pe.wait_ge(mixture_low_ready, B)
                pe.matmul(zbank[:, 0:L], last_mixT[:, P:2 * P], ow[:, 1, :], start=False,
                          stop=True).then_inc(projected, 1)

            def project(b):
                if b == 0:
                    pe.wait_ge(out_weights_low_ready, 1)
                if b:
                    pe.wait_ge(y_ready, b)
                pe.wait_ge(mixture_low_ready, b + 1)
                for c in range(C):
                    hi, lo = mixT_hi[:, b % 2, P * c:P * (c + 1)], mixT_lo[:, b % 2, P * c:P * (c + 1)]
                    pe.matmul(zbank[:, 0:L], hi, ow_hi[:, c, :], start=(c == 0), stop=False)
                    pe.matmul(zbank[:, 0:L], hi, ow_lo[:, c, :], start=False, stop=False)
                    last = pe.matmul(zbank[:, 0:L], lo, ow_hi[:, c, :], start=False, stop=(c == C - 1))
                last.then_inc(projected, 1)

            warm_up(WARM_UP[0], ring[RING - 1])
            for i in range(LOADS):
                context(i)
                warm_up(WARM_UP[i + 1], ring[RING - 1])
            for n in range(2 * H):
                convolve(n)
                if n == 0:
                    queries(0)
                    queries(1)
                if n == 14:
                    queries(2)
                if n == 15:
                    queries(3)
                for i in due(SUMS, n):
                    sum_channels(i)
                for i in due(ZTS, n):
                    z_transposed(i)
            for j, (b, k) in enumerate(BLOCKS):
                experts(j, b, k)
                for i in due(LATE_SUMS, j):
                    sum_channels(BG + i)
                for i in due(LATE_ZTS, j):
                    z_transposed(BG + i)
                if j == 0:
                    route_logits(0)
                if j == 1:
                    route_rows(0)
                if j == LATE_ROUTE:
                    route_logits(1)
                if j == LATE_ROUTE + 1:
                    route_rows(1)
                for i in due(MIXED, j - PROJECTED):
                    project(i)
                for i in due(MIXED, j):
                    mix_transposed(i)
            project(B - 2)
            warm_up(WARM_UP[-1], red[0])
            last_mixture()

        @block.vector
        def _(dve):
            def statistics(b):
                dve.bn_stats(stats[:, 6 * b:6 * (b + 1)], xv[:, b, :]).then_inc(row_stats_ready, 1)
                dve.wait_ge(row_stats_ready, b + 1)
                dve.bn_aggr(mvv[:, b, :], stats[:, 6 * b:6 * (b + 1)]).then_inc(moments_ready, 1)

            def query_scales():
                dve.wait_ge(inverse_std_ready, 1)
                dve.wait_ge(tanh_ready, 1)
                dve.tensor_scalar(qscale[:, 0:BG], rstd[:, 0:BG], tgains[:, 0:1], None,
                                  ALU.mult).then_inc(first_query_scales_ready, 1)

            def evacuate_queries():
                dve.wait_ge(queries_transposed, 2)
                dve.tensor_copy(qT[:, 0, :, BL:BG, :].rearrange("p c b n -> p c (b n)"),
                                obank[:, :].rearrange("p (c n) -> p c n", c=C)).then_inc(dve_queries_evacuated, 1)

            def queries(i):
                dve.wait_ge(first_query_scales_ready, 1)
                for b in range(BL * i, BL * (i + 1)):
                    dve.tensor_scalar(backwards(q_t, B * L, b * L), xv[:, b, :].rearrange("p (c n) -> p c n", c=C),
                                      mvv[:, b, 0:1], qscale[:, b:b + 1], ALU.subtract,
                                      ALU.mult).then_inc(first_queries_ready, 1)

            def query_products(n):
                g, h = divmod(n, H)
                if h == 0:
                    dve.wait_ge(act_queries_evacuated, 2 * g + 1)
                    dve.wait_ge(dve_queries_evacuated, 1)
                dve.wait_ge(convolved, n + 1)
                y = ring[n % RING][:, 0:CB * NP].rearrange("p (a n) -> p a n", a=CB)
                rows_lo = y[:, :, 0:NPU].rearrange("p a (i j) -> p a i j", i=HB)
                rows_hi = y[:, :, NPU:NP].rearrange("p a (i j) -> p a i j", i=HB)
                q = qTm[:, g, :, HD * h:HD * (h + 1)]
                dst = zq[:, g, :, :, HD * h:HD * (h + 1)]
                dve.tensor_tensor(dst[:, :, 0:HB, :], rows_lo, q[:, :, 0:HB].unsqueeze(3).to_broadcast([P, CB, HB, HD]),
                                  ALU.mult)
                q_hi = q[:, :, HB:HD].unsqueeze(3).to_broadcast([P, CB, HB, HB])
                dve.tensor_tensor(dst[:, :, HB:HD, HB:HD], rows_hi, q_hi, ALU.mult)
                dve.tensor_tensor(dst[:, :, HB:HD, 0:HB], rows_lo[:, :, :, HB:HD].rearrange("p a i j -> p a j i"), q_hi,
                                  ALU.mult).then_inc(read_out, 1)

            def residual(b):
                dve.wait_ge(summed, b + 1)
                row = xv[:, b, :].rearrange("p (c n) -> p c n", c=C)
                dve.tensor_tensor(row, backwards(red[b % 2], 512, 0), row, ALU.add).then_inc(x1_ready, 1)

            def z_low(b):
                dve.wait_ge(z_high_ready, b + 1)
                dve.tensor_tensor(zT_lo[:, b].rearrange("p c n -> p (c n)"), zbanks[b % 2][:, 0:L],
                                  zT_hi[:, b].rearrange("p c n -> p (c n)").bitcast(F32),
                                  ALU.subtract).then_inc(z_low_ready, 1)

            def projection_low():
                dve.wait_ge(out_weights_high_ready, 1)
                dve.tensor_tensor(ow_lo_t[:, :], ow_t[:, :], ow_hi_t[:, :].bitcast(F32),
                                  ALU.subtract).then_inc(out_weights_low_ready, 1)

            def mix_low(b):
                dve.wait_ge(mixture_high_ready, b + 1)
                dve.tensor_tensor(mixT_lo[:, b % 2], obank[:, 0:C * P], mixT_hi[:, b % 2].bitcast(F32),
                                  ALU.subtract).then_inc(mixture_low_ready, 1)

            def router_split():
                dve.wait_ge(router_relative, 1)
                dve.tensor_copy(rw_hi[:, :], rw_t[:, :]).then_inc(router_split_ready, 1)
                dve.wait_ge(router_split_ready, 1)
                dve.tensor_tensor(rw_lo[:, :], rw_t[:, :], rw_hi[:, :].bitcast(F32),
                                  ALU.subtract).then_inc(router_split_ready, 1)

            def choose(g):
                dve.wait_ge(logit_rows_evacuated, g + 1)
                for b in range(BG):
                    dve.max(topv[:, b, :], lgv[:, b, :]).then_inc(tops_ready, 1)
                dve.wait_ge(tops_ready, BG * (g + 1))
                if g:
                    dve.wait_ge(gap_tanh_ready, g)
                dve.tensor_tensor(gap[:, :], topv[:, :, 0], topv[:, :, 1], ALU.subtract).then_inc(gap_ready, 1)
                for b in range(BG):
                    last = dve.max_index(topiv[:, b, :], topv[:, b, :], lgv[:, b, :])
                last.then_inc(indices_ready, 1)
                dve.wait_ge(indices_ready, 2 * g + 1)
                dve.tensor_copy(topfv, topiv[:, :, 0:2]).then_inc(indices_ready, 1)

            def weigh(g):
                dve.wait_ge(gap_tanh_ready, g + 1)
                dve.wait_ge(gain_terms_ready, 2)
                dve.tensor_scalar(gate2[:, 0:BG], tgap[:, :], halfg[:, 0:1], halfg[:, 0:1], ALU.mult,
                                  ALU.add).then_inc(gate_pair_ready, 1)
                dve.tensor_scalar(gate2[:, BG:2 * BG], tgap[:, :], halfg[:, 1:2], halfg[:, 0:1], ALU.mult,
                                  ALU.add).then_inc(gate_pair_ready, 1)
                dve.wait_ge(indices_ready, 2 * g + 2)
                for k in range(2):
                    dve.tensor_tensor(hitv[:, k], eids[:, :].unsqueeze(1).to_broadcast([P, BG, E]),
                                      topfv[:, :, k:k + 1].to_broadcast([P, BG, E]),
                                      ALU.is_equal).then_inc(hits_ready, 1)
                dve.wait_ge(gate_pair_ready, 2 * g + 2)
                dve.wait_ge(hits_ready, 4 * g + 2)
                for k in range(2):
                    dve.tensor_tensor(hitv[:, k], hitv[:, k],
                                      gate2[:, BG * k:BG * (k + 1)].unsqueeze(2).to_broadcast([P, BG, E]),
                                      ALU.mult).then_inc(hits_ready, 1)
                dve.wait_ge(hits_ready, 4 * g + 4)
                dve.tensor_tensor(gates[:, BG * g:BG * (g + 1), :], hitv[:, 0], hitv[:, 1],
                                  ALU.add).then_inc(gates_ready, 1)

            def accumulate(n, b, k):
                dve.wait_ge(gelu_ready, n + 1)
                if k == 0 and b % BG == 0:
                    dve.wait_ge(gates_ready, b // BG + 1)
                if k == 0 and b >= BG:
                    dve.wait_ge(mixture_transposed, b - BG + 1)
                acc = mix[:, b % BG, :]
                for e in range(2):
                    gate = gates[:, b, 2 * k + e:2 * k + e + 1]
                    if n == len(BLOCKS) - 1 and e == 1:
                        dve.wait_ge(gelu_ready, n + 2)
                        dve.wait_ge(mixed_in, 2 * n + 1)
                        for c in range(C):
                            half = acc[:, P * c:P * (c + 1)]
                            dve.scalar_tensor_tensor(out=half, in0=ring[(n + 1) % RING][:, P * c:P * (c + 1)],
                                                     scalar=gate, in1=half, op0=ALU.mult, op1=ALU.add).then_inc(mixed_in, 1)
                    elif k == 0 and e == 0:
                        dve.tensor_scalar(acc, ring[n % RING][:, 0:L], gate, None, ALU.mult).then_inc(mixed_in, 1)
                    else:
                        dve.wait_ge(mixed_in, 2 * n + 1 if e else added(b, k - 1))
                        dve.scalar_tensor_tensor(out=acc, in0=ring[n % RING][:, L * e:L * (e + 1)], scalar=gate,
                                                 in1=acc, op0=ALU.mult, op1=ALU.add).then_inc(mixed_in, 1)

            def finish(b):
                dve.wait_ge(projected, b + 1)
                dve.wait_ge(bias_added, b + 1)
                dve.tensor_tensor(xv[:, b, :], zbank[:, 0:L], xv[:, b, :], ALU.add).then_inc(y_ready, 1)

            dve.wait_ge(taps_in, 32)
            dve.tensor_copy(kpad[:, 0:L - 1], bass.AP(mix_t, L - 1, [[BG * L, H], [-1, L - 1]]))
            dve.tensor_tensor(kpad[:, L - 1:L], taps[:, 0:1], dcol[:, :], ALU.add).then_inc(taps_reversed, 1)
            for b in range(BG):
                if b % BL == 0:
                    dve.wait_ge(x_in[b // BL], 16)
                statistics(b)
            dve.wait_ge(moments_ready, BG)
            dve.tensor_scalar(vareps[:, 0:BG], mvv[:, :, 1], EPS, None, ALU.add).then_inc(first_variances_ready, 1)
            products(dve, 0, dve_products_ready)
            query_scales()
            queries(0)
            queries(1)
            evacuate_queries()
            for n in range(2 * H):
                if by_vector(n + 3):
                    products(dve, n + 3, dve_products_ready)
                query_products(n)
                for i in due(HALVES, n):
                    halve_sum(dve, HALVED_BY_DVE[i], dve_halved)
                if n == ROUTER_SPLIT:
                    router_split()
                for i in due(SUMS, n - 1):
                    residual(i)
                for i in due(ZTS, n):
                    z_low(i)
            for b in HALVED_BY_DVE[len(HALVES):]:
                halve_sum(dve, b, dve_halved)
            projection_low()
            dve.tensor_scalar(halfg[:, 0:1], tgains[:, 1:2], 0.5, None, ALU.mult).then_inc(gain_terms_ready, 1)
            dve.tensor_scalar(halfg[:, 1:2], tgains[:, 1:2], -0.5, None, ALU.mult).then_inc(gain_terms_ready, 1)
            dve.wait_ge(out_bias_in, 16)
            dve.tensor_scalar(obias[:, :], obias[:, :], tgains[:, 1:2], None, ALU.mult).then_inc(gain_terms_ready, 1)
            residual(BG)
            choose(0)
            weigh(0)
            for j, (b, k) in enumerate(BLOCKS):
                for i in due(LATE_SUMS[1:], j):
                    residual(BG + i + 1)
                for i in due(LATE_ZTS, j):
                    z_low(BG + i)
                accumulate(j, b, k)
                if j == LATE_ROUTE + 1:
                    choose(1)
                if j == LATE_ROUTE + 2:
                    weigh(1)
                for i in due(MIXED, j - PROJECTED):
                    finish(i)
                for i in due(MIXED, j):
                    mix_low(i)
            finish(B - 2)
            dve.wait_ge(mixture_transposed, B + 1)
            dve.tensor_copy(last_mixT[:, P:2 * P], red[1][:, 0:P]).then_inc(mixture_low_ready, 1)
            finish(B - 1)


_INS = ["x", "ctx_2048", "g_xattn", "g_ffn", "L0_xattn_ssm_kernel", "L0_xattn_D", "L0_ffn_router_w", "L0_ffn_router_b",
        "L0_ffn_expert_w", "L0_ffn_expert_b", "L0_ffn_out_w", "L0_ffn_out_b"]


def kernel(**inputs):
    import numpy as _np
    import concourse.bacc as _bacc
    from concourse import mybir as _mybir
    from concourse.bass_utils import run_bass_kernel_spmd as _run

    nc = _bacc.Bacc("TRN2", target_bir_lowering=False, num_devices=1)
    arrays, args = {}, []
    for name in _INS:
        a = _np.ascontiguousarray(inputs[name])
        arrays[f"in_{name}"] = a
        args.append(nc.dram_tensor(f"in_{name}", a.shape, _mybir.dt.from_np(a.dtype), kind="ExternalInput").ap())
    shape = inputs["x"].shape
    args.append(nc.dram_tensor("out_0", shape, _mybir.dt.float32, kind="ExternalOutput").ap())
    flamingo_kernel(nc, *args)
    r = _run(nc, [arrays], core_ids=[0])
    return r.results[0]["out_0"]
```
